# Optimizing a Trainium2 kernel written in Bass

```python
import numpy as np
import jax
import jax.numpy as jnp

def _softmax(x, axis=-1):
    return jax.nn.softmax(x, axis=axis)

def _gelu(x):
    return jax.nn.gelu(x, approximate=True)

def _silu(x):
    return jax.nn.silu(x)

def _sigmoid(x):
    return jax.nn.sigmoid(x)

def _layernorm(x, axis=-1, eps=1e-05):
    m = jnp.mean(x, axis=axis, keepdims=True)
    v = jnp.var(x, axis=axis, keepdims=True)
    return (x - m) / jnp.sqrt(v + eps)

def _scatter_add(tgt, idx, src, axis=0):
    return tgt.at[idx].add(src)

def _segment_sum(src, seg, n):
    return jax.ops.segment_sum(src, seg, n)
kernel_name = 'mk_audio_tower_d1_tok_audfeat512_r4_da64d0'

def setup_inputs(seed: int=0):
    np.random.seed(seed)
    _w = jnp.asarray

    def _rec_inputs():
        import jax
        import jax.numpy as jnp
        _rk = jax.random.key(seed)
        x = 7.22013e-05 + 1.00017 * jax.random.normal(jax.random.fold_in(_rk, 1), (16, 375, 128), jnp.float32)
        return x
    x = _rec_inputs()

    def _L0_tok_setup():
        import jax, jax.numpy as jnp
        import numpy as np
        B, T, D, H, K = (16, 256, 128, 128, 2)
        key = jax.random.key(seed)
        ks = jax.random.split(key, 7)
        scale = 1.0 / np.sqrt(D * K)
        x = jax.random.normal(ks[0], (B, T, D), dtype=jnp.float32)
        W_z = jax.random.uniform(ks[1], (H, D, K), jnp.float32, -scale, scale)
        b_z = jax.random.uniform(ks[2], (H,), jnp.float32, -scale, scale)
        W_f = jax.random.uniform(ks[3], (H, D, K), jnp.float32, -scale, scale)
        b_f = jax.random.uniform(ks[4], (H,), jnp.float32, -scale, scale)
        W_o = jax.random.uniform(ks[5], (H, D, K), jnp.float32, -scale, scale)
        b_o = jax.random.uniform(ks[6], (H,), jnp.float32, -scale, scale)
        return {'x': x, 'W_z': W_z, 'b_z': b_z, 'W_f': W_f, 'b_f': b_f, 'W_o': W_o, 'b_o': b_o}
    _L0_tok_all = _L0_tok_setup()
    _L0_tok_in = {k: v for k, v in _L0_tok_all.items() if k in ('W_z', 'b_z', 'W_f', 'b_f', 'W_o', 'b_o')}
    del _L0_tok_all

    def _L0_attn_setup():
        import jax, jax.numpy as jnp
        import numpy as np
        import math
        _DENSE_LOCAL_W = 32
        _DYADIC = [48, 64, 96, 128, 192, 64, 96, 128, 192, 256, 384, 512, 768, 1024]
        OFFSETS = np.array(sorted(set(range(0, _DENSE_LOCAL_W + 1)) | set(_DYADIC)), dtype=np.int32)
        NUM_OFFSETS = len(OFFSETS)
        H = 8
        _LOG_MAX = math.log(1.0 + 4096.0)
        _HEAD_OMEGAS = [0.0, 0.0, 1 * math.pi / _LOG_MAX, 1 * math.pi / _LOG_MAX, 4 * math.pi / _LOG_MAX, 4 * math.pi / _LOG_MAX, 6 * math.pi / _LOG_MAX, 6 * math.pi / _LOG_MAX]
        _log_d = np.log(1.0 + OFFSETS.astype(np.float64))
        _CK = np.zeros((NUM_OFFSETS, H), dtype=np.float32)
        for _h, _om in enumerate(_HEAD_OMEGAS):
            if _om > 0.0:
                _CK[:, _h] = np.cos(_om * _log_d)
        DISP_COS_KERNEL = jnp.asarray(_CK)
        B, N, D = (1, 512, 128)
        HD = D // H
        key = jax.random.key(seed)
        ks = jax.random.split(key, 8)
        s = 0.02
        return {'x': jax.random.normal(ks[0], (B, N, D), jnp.float32), 'W_qkv': jax.random.normal(ks[1], (D, 3 * D), jnp.float32) * s, 'b_qkv': jax.random.normal(ks[2], (3 * D,), jnp.float32) * s, 'W_out': jax.random.normal(ks[3], (D, D), jnp.float32) * s, 'b_out': jax.random.normal(ks[4], (D,), jnp.float32) * s, 'W_gate': jax.random.normal(ks[5], (D, D), jnp.float32) * s, 'b_gate': jnp.zeros((D,), jnp.float32), 'pos_bias': jnp.zeros((NUM_OFFSETS, H), jnp.float32) + 0.001, 'scale_embed': jnp.zeros((NUM_OFFSETS, HD), jnp.float32), 'if_gain': jnp.ones((H,), jnp.float32), 'disp_amp': jnp.full((H,), 0.1, jnp.float32)}
    _L0_attn_all = _L0_attn_setup()
    _L0_attn_in = {k: v for k, v in _L0_attn_all.items() if k in ('W_qkv', 'b_qkv', 'W_out', 'b_out', 'W_gate', 'b_gate', 'pos_bias', 'scale_embed', 'if_gain', 'disp_amp')}
    del _L0_attn_all

    def _L0_ffn_setup():
        import jax, jax.numpy as jnp
        import numpy as np
        E = 64
        K = 2
        CAP = 128
        H = 128
        FFN = 512
        B, S = (8, 1024)
        key = jax.random.key(seed)
        ks = jax.random.split(key, 6)
        hidden_states = jax.random.normal(ks[0], (B, S, H), dtype=jnp.float32)
        router_w = jax.random.normal(ks[1], (E, H), dtype=jnp.float32) * (0.01 / np.sqrt(H))
        w1 = jax.random.normal(ks[2], (FFN, H), dtype=jnp.float32) * (1.0 / np.sqrt(H))
        b1 = jnp.zeros((FFN,), dtype=jnp.float32)
        w2 = jax.random.normal(ks[3], (H, FFN), dtype=jnp.float32) * (1.0 / np.sqrt(FFN))
        b2 = jnp.zeros((H,), dtype=jnp.float32)
        return {'hidden_states': hidden_states, 'router_w': router_w, 'w1': w1, 'b1': b1, 'w2': w2, 'b2': b2}
    _L0_ffn_all = _L0_ffn_setup()
    _L0_ffn_in = {k: v for k, v in _L0_ffn_all.items() if k in ('router_w', 'w1', 'b1', 'w2', 'b2')}
    del _L0_ffn_all
    return {'x': x, 'L0_tok_W_z': _L0_tok_in['W_z'], 'L0_tok_b_z': _L0_tok_in['b_z'], 'L0_tok_W_f': _L0_tok_in['W_f'], 'L0_tok_b_f': _L0_tok_in['b_f'], 'L0_tok_W_o': _L0_tok_in['W_o'], 'L0_tok_b_o': _L0_tok_in['b_o'], 'L0_attn_W_qkv': _L0_attn_in['W_qkv'], 'L0_attn_b_qkv': _L0_attn_in['b_qkv'], 'L0_attn_W_out': _L0_attn_in['W_out'], 'L0_attn_b_out': _L0_attn_in['b_out'], 'L0_attn_W_gate': _L0_attn_in['W_gate'], 'L0_attn_b_gate': _L0_attn_in['b_gate'], 'L0_attn_pos_bias': _L0_attn_in['pos_bias'], 'L0_attn_scale_embed': _L0_attn_in['scale_embed'], 'L0_attn_if_gain': _L0_attn_in['if_gain'], 'L0_attn_disp_amp': _L0_attn_in['disp_amp'], 'L0_ffn_router_w': _L0_ffn_in['router_w'], 'L0_ffn_w1': _L0_ffn_in['w1'], 'L0_ffn_b1': _L0_ffn_in['b1'], 'L0_ffn_w2': _L0_ffn_in['w2'], 'L0_ffn_b2': _L0_ffn_in['b2']}

def reference(x, L0_tok_W_z, L0_tok_b_z, L0_tok_W_f, L0_tok_b_f, L0_tok_W_o, L0_tok_b_o, L0_attn_W_qkv, L0_attn_b_qkv, L0_attn_W_out, L0_attn_b_out, L0_attn_W_gate, L0_attn_b_gate, L0_attn_pos_bias, L0_attn_scale_embed, L0_attn_if_gain, L0_attn_disp_amp, L0_ffn_router_w, L0_ffn_w1, L0_ffn_b1, L0_ffn_w2, L0_ffn_b2):
    import jax
    import jax.numpy as jnp

    def _L0_tok_ref(x, W_z, b_z, W_f, b_f, W_o, b_o):
        import jax, jax.numpy as jnp
        import numpy as np
        B, T, D, H, K = (16, 256, 128, 128, 2)

        def conv(W, b):
            return jnp.einsum('btd,hd->bth', x[:, :-1, :], W[:, :, 0]) + jnp.einsum('btd,hd->bth', x[:, 1:, :], W[:, :, 1]) + b
        z = jnp.tanh(conv(W_z, b_z))
        f = jax.nn.sigmoid(conv(W_f, b_f))
        o = jax.nn.sigmoid(conv(W_o, b_o))

        def step(c, zfo):
            zt, ft, ot = zfo
            c = ft * c + (1.0 - ft) * zt
            return (c, ot * c)
        c0 = jnp.zeros_like(z[:, 0, :])
        zT = jnp.swapaxes(z, 0, 1)
        fT = jnp.swapaxes(f, 0, 1)
        oT = jnp.swapaxes(o, 0, 1)
        _, h = jax.lax.scan(step, c0, (zT, fT, oT))
        return jnp.swapaxes(h, 0, 1)

    def _L0_attn_ref(x, W_qkv, b_qkv, W_out, b_out, W_gate, b_gate, pos_bias, scale_embed, if_gain, disp_amp):
        import jax, jax.numpy as jnp
        import numpy as np
        import math
        _DENSE_LOCAL_W = 32
        _DYADIC = [48, 64, 96, 128, 192, 64, 96, 128, 192, 256, 384, 512, 768, 1024]
        OFFSETS = np.array(sorted(set(range(0, _DENSE_LOCAL_W + 1)) | set(_DYADIC)), dtype=np.int32)
        NUM_OFFSETS = len(OFFSETS)
        H = 8
        _LOG_MAX = math.log(1.0 + 4096.0)
        _HEAD_OMEGAS = [0.0, 0.0, 1 * math.pi / _LOG_MAX, 1 * math.pi / _LOG_MAX, 4 * math.pi / _LOG_MAX, 4 * math.pi / _LOG_MAX, 6 * math.pi / _LOG_MAX, 6 * math.pi / _LOG_MAX]
        _log_d = np.log(1.0 + OFFSETS.astype(np.float64))
        _CK = np.zeros((NUM_OFFSETS, H), dtype=np.float32)
        for _h, _om in enumerate(_HEAD_OMEGAS):
            if _om > 0.0:
                _CK[:, _h] = np.cos(_om * _log_d)
        DISP_COS_KERNEL = jnp.asarray(_CK)
        B, N, D = (1, 512, 128)
        HD = D // H
        Bx, Nx, Dx = x.shape
        qkv = x @ W_qkv + b_qkv
        q, k, v = jnp.split(qkv, 3, axis=-1)
        q = q.reshape(Bx, Nx, H, HD).transpose(0, 2, 1, 3)
        k = k.reshape(Bx, Nx, H, HD).transpose(0, 2, 1, 3)
        v = v.reshape(Bx, Nx, H, HD).transpose(0, 2, 1, 3)
        deltas = jnp.asarray(OFFSETS)
        pos = jnp.arange(Nx)
        j = pos[None, :] - deltas[:, None]
        valid = j >= 0
        jc = jnp.maximum(j, 0)
        kg = k[:, :, jc]
        vg = v[:, :, jc]
        km = kg * (1.0 + scale_embed)[None, None, :, None, :]
        eff_pb = pos_bias + DISP_COS_KERNEL * disp_amp[None, :]
        scores = jnp.einsum('bhnd,bhond->bhon', q, km) / math.sqrt(HD)
        scores = scores + eff_pb.T[None, :, :, None]
        scores = jnp.where(valid[None, None], scores, -jnp.inf)
        attn = jax.nn.softmax(scores, axis=2)
        out = jnp.einsum('bhon,bhond->bhnd', attn, vg)
        out = out * if_gain[None, :, None, None]
        out_flat = out.transpose(0, 2, 1, 3).reshape(Bx, Nx, Dx)
        gate = jax.nn.sigmoid(x @ W_gate + b_gate)
        return out_flat * gate @ W_out + b_out

    def _L0_ffn_ref(hidden_states, router_w, w1, b1, w2, b2):
        import jax, jax.numpy as jnp
        import numpy as np
        E = 64
        K = 2
        CAP = 128
        H = 128
        FFN = 512
        B, S = (8, 1024)
        orig_shape = hidden_states.shape
        x = hidden_states.reshape(-1, orig_shape[-1])
        T = x.shape[0]
        N = T * K
        logits = jnp.einsum('th,eh->te', x, router_w)
        probs_full = jax.nn.softmax(logits, axis=-1)
        probs, idx = jax.lax.top_k(probs_full, K)
        flat_e = idx.reshape(-1)
        flat_p = probs.reshape(-1)
        order = jnp.argsort(flat_e, stable=True)
        sorted_e = flat_e[order]
        counts = jnp.zeros((E,), jnp.int32).at[flat_e].add(1)
        offsets = jnp.concatenate([jnp.zeros((1,), jnp.int32), jnp.cumsum(counts)[:-1]])
        pos = jnp.arange(N, dtype=jnp.int32) - offsets[sorted_e]
        keep = pos < CAP
        slot = sorted_e * CAP + jnp.minimum(pos, CAP - 1)
        dest = jnp.where(keep, slot, E * CAP)
        tok = order // K
        buf = jnp.zeros((E * CAP + 1, x.shape[-1]), x.dtype).at[dest].set(x[tok])
        buf = buf[:-1]
        h = jax.nn.gelu(jnp.einsum('nh,fh->nf', buf, w1) + b1, approximate=False)
        y = jnp.einsum('nf,hf->nh', h, w2) + b2
        gate = jnp.where(keep, flat_p[order], 0.0)
        contrib = y[jnp.minimum(slot, E * CAP - 1)] * gate[:, None]
        out = jnp.zeros_like(x).at[tok].add(contrib)
        return out.reshape(orig_shape)
    h = _L0_tok_ref(x, L0_tok_W_z, L0_tok_b_z, L0_tok_W_f, L0_tok_b_f, L0_tok_W_o, L0_tok_b_o)
    h = h + _L0_attn_ref(_layernorm(h, axis=-1), L0_attn_W_qkv, L0_attn_b_qkv, L0_attn_W_out, L0_attn_b_out, L0_attn_W_gate, L0_attn_b_gate, L0_attn_pos_bias, L0_attn_scale_embed, L0_attn_if_gain, L0_attn_disp_amp)
    h = h + _L0_ffn_ref(_layernorm(h, axis=-1), L0_ffn_router_w, L0_ffn_w1, L0_ffn_b1, L0_ffn_w2, L0_ffn_b2)
    return h

_drawn_inputs = setup_inputs


def setup_inputs(seed=0):
    import zlib

    import numpy as np

    out = dict(_drawn_inputs(seed))
    spreads = {'L0_attn_b_gate': (0.0, 2.0),
     'L0_attn_pos_bias': (0.0010000000474974513, 0.6),
     'L0_attn_scale_embed': (0.0, 2.0),
     'L0_attn_if_gain': (1.0, 0.6),
     'L0_attn_disp_amp': (0.10000000149011612, 0.6),
     'L0_ffn_b1': (0.0, 0.713),
     'L0_ffn_b2': (0.0, 0.479)}
    factors = {'L0_tok_b_f': 3.096, 'L0_tok_b_o': 2.947, 'L0_attn_W_gate': 6.403}
    for name, (base, spread) in spreads.items():
        noise = np.random.default_rng([zlib.crc32(name.encode()), seed]).standard_normal(out[name].shape)
        drawn = base * np.exp(spread * noise) if base else spread * noise
        out[name] = jnp.asarray(drawn.astype(out[name].dtype))
    for name, factor in factors.items():
        out[name] = (out[name] * factor).astype(out[name].dtype)
    return out
```

```python
import numpy as np
import concourse.bass as bass
from concourse import mybir
from contextlib import ExitStack

BATCH, ROWS, D = 16, 375, 128
N = ROWS - 1
NP = 384
TT = NP // 128
BT, NB = 96, NP // 96
HEADS, HD = 8, 16
LOCAL = 32
DENSE = LOCAL + 1
FAR = [48, 64, 96, 128, 192, 256]
NFAR = len(FAR)
OFFS = [LOCAL - j for j in range(DENSE)] + FAR
NO = len(OFFS)
CW = 16
CH = NO // CW
LAST = NO - CH * CW
KPAD = max(FAR)
SC = HEADS * NO
EXPERTS, TOPK, CAP, FFN = 64, 2, 128, 512
FC = FFN // 128
EPS = 1e-5
MASKED = -1e30
XT = 125

FIELDS = [
    ("ident", 128), ("conv", 6 * D), ("bias", 12), ("cen", 128), ("cen4", 128), ("avg", 128),
    ("qkv", 3 * D), ("gatew", D),
    ("se", NO), ("ind", 4 * 32), ("amp", HEADS), ("gain", HEADS), ("pick", NFAR * 128), ("outw", D), ("router", EXPERTS), ("up", FFN), ("down", FC * D), ("b2", D),
    ("iota", EXPERTS), ("before", 128), ("ones", 128),
]
SETUP = [("pos", SC), ("cosk", SC), ("mask", TT * NO)]
COL, _at = {}, 0
for _n, _w in FIELDS:
    COL[_n] = (_at, _at + _w)
    _at += _w
PCOLS = _at
for _n, _w in SETUP:
    COL[_n] = (_at, _at + _w)
    _at += _w
ALLCOLS = _at
BZ, BF, BO, BQ, BK, BV, BG, BOUT, B1 = 0, 1, 2, 3, 4, 5, 6, 7, 8


class Seq:

    def __init__(self, b, s, g):
        self.b, self.s, self.g = b, s, g


def build(nc, x, params, out):
    fp32, bf16, u32 = mybir.dt.float32, mybir.dt.bfloat16, mybir.dt.uint32
    ALU, ACT, AX = mybir.AluOpType, mybir.ActivationFunctionType, mybir.AxisListType
    band_dram = nc.dram_tensor("band_scratch", [2, NP, HEADS * 128], fp32, kind="Internal").ap()

    with ExitStack() as ctx:
        def sb(name, shape, dt=fp32):
            return ctx.enter_context(nc.sbuf_tensor(name, shape, dt))

        def bank(name):
            return ctx.enter_context(nc.psum_tensor(name, [128, 512], fp32))

        def sem(name):
            return ctx.enter_context(nc.semaphore(name))

        par = sb("par", [128, PCOLS])

        def P(name, a=0, b=None):
            lo, hi = COL[name]
            if lo >= PCOLS:
                flat = attn[0][:, :, :, :].rearrange("p t h o -> p (t h o)")
                return flat[:, lo - PCOLS + a:(hi if b is None else lo + b) - PCOLS]
            return par[:, lo + a:(hi if b is None else lo + b)]

        xin = [sb(f"xin{s}", [XT, 3, D]) for s in range(2)]
        xT = sb("xT", [128, NP + 1])
        zt, ft, ot = sb("zt", [128, NP]), sb("ft", [128, NP]), sb("ot", [128, NP])
        forget, mixin, cell = sb("forget", [128, NP]), sb("mixin", [128, NP]), sb("cell", [128, NP])
        back4 = sb("back4", [128, 1])
        h = [sb(f"h{s}", [128, NP]) for s in range(2)]
        hkeep = [sb(f"hkeep{s}", [128, NP]) for s in range(2)]
        sq, lnv, rstd = sb("sq", [128, NP]), sb("lnv", [128, NP]), sb("rstd", [128, NP])
        xn = [sb(f"xn{s}", [128, NP]) for s in range(2)]
        q = [sb(f"q{s}", [128, NP]) for s in range(2)]
        k = [sb(f"k{s}", [128, KPAD + NP]) for s in range(2)]
        vT = [sb(f"vT{s}", [128, LOCAL + NP]) for s in range(2)]
        gate = [sb(f"gate{s}", [128, NP]) for s in range(2)]
        prod = [sb(f"prod{c}", [128, CW, N]) for c in range(CH)]
        fprod = sb("fprod", [128, LAST, N])
        ew = sb("ew", [128, NO, 32])
        scT = sb("scT", [128, CH + 1, NP])
        bm = sb("bm", [128, TT, HEADS, NO])
        sc = sb("sc", [128, TT * HEADS, NO])
        ex = sb("ex", [128, TT * HEADS, NO])
        mx, sm, rs = sb("mx", [128, TT * HEADS]), sb("sm", [128, TT * HEADS]), sb("rs", [128, TT * HEADS])
        attn = [sb(f"attn{s}", [128, TT, HEADS, DENSE]) for s in range(2)]
        attnf = [sb(f"attnf{s}", [128, TT, HEADS * NFAR]) for s in range(2)]
        band = sb("band", [BT, NB, HEADS * 128])
        bandT = [sb(f"bandT{i}", [128, 4 * BT]) for i in range(2)]
        v2 = sb("v2", [128, NB, HEADS, 32])
        farT = sb("farT", [HEADS * NFAR, NP])
        acc = sb("acc", [128, NP])
        tmp = [sb(f"tmp{i}", [128, NP]) for i in range(2)]
        o1, ao, h2 = sb("o1", [128, NP]), sb("ao", [128, NP]), sb("h2", [128, NP])
        sq2, lnv2, rstd2, x2 = (sb(n, [128, NP]) for n in ("sq2", "lnv2", "rstd2", "x2"))
        lg, lsub, exr = (sb(n, [128, TT, EXPERTS]) for n in ("lg", "lsub", "exr"))
        m8 = sb("m8", [128, TT, 8])
        i8 = sb("i8", [128, TT, 8], u32)
        idf = sb("idf", [128, TT, TOPK])
        eq0, eq1 = sb("eq0", [128, TT, EXPERTS]), sb("eq1", [128, TT, EXPERTS])
        msk = sb("msk", [128, TT, EXPERTS], bf16)
        room = sb("room", [128, EXPERTS])
        kept, kw = sb("kept", [128, TT, EXPERTS]), sb("kw", [128, TT, EXPERTS])
        lmax, gs, smr, rcr, gt = (sb(n, [128, TT]) for n in ("lmax", "gs", "smr", "rcr", "gt"))
        beforeb, onesb = sb("beforeb", [128, 128], bf16), sb("onesb", [128, 128], bf16)
        hid = sb("hid", [128, FC, NP])
        y1 = sb("y1", [128, TT, D])
        osb = [sb(f"osb{s}", [128, TT, D]) for s in range(2)]
        hbias = sb("hbias", [128, 12])
        epsc = sb("epsc", [128, 1])
        se1 = sb("se1", [128, NO])
        gain2 = sb("gain2", [128, HEADS])
        bias_oh = attn[1][:, :, :, :].rearrange("p t h o -> p (t h o)")[:, 0:SC].rearrange("p (h o) -> p h o", o=NO)

        T0, T1 = bank("T0"), bank("T1")
        S = [bank(f"S{t}") for t in range(TT)]
        V0, V1, V2 = bank("V0"), bank("V1"), bank("V2")

        par_in, pads_zero, scratch_zero = sem("par_in"), sem("pads_zero"), sem("scratch_zero")
        setup_dve, setup_lin, x_turned = sem("setup_dve"), sem("setup_lin"), sem("x_turned")
        xT_ready, z_mm, z_ready = sem("xT_ready"), sem("z_mm"), sem("z_ready")
        f_mm, f_ready, o_mm = sem("f_mm"), sem("f_ready"), sem("o_mm")
        o_ready, mixin_ready, c_ready = sem("o_ready"), sem("mixin_ready"), sem("c_ready")
        h_ready, hc_mm, sq_ready = sem("h_ready"), sem("hc_mm"), sem("sq_ready")
        var_mm, lnv_ready, rstd_ready = sem("var_mm"), sem("lnv_ready"), sem("rstd_ready")
        xn_ready, q_mm, q_ready = sem("xn_ready"), sem("q_mm"), sem("q_ready")
        k_mm, k_ready, v_mm = sem("k_mm"), sem("k_ready"), sem("v_mm")
        v_ready, gate_mm, gate_ready = sem("v_ready"), sem("gate_mm"), sem("gate_ready")
        hkeep_ready, scores_mm, sc_ready = sem("hkeep_ready"), sem("scores_mm"), sem("sc_ready")
        mx_ready, sub_ready, ex_ready = sem("mx_ready"), sem("sub_ready"), sem("ex_ready")
        sm_ready, rc_ready, rs_ready = sem("sm_ready"), sem("rc_ready"), sem("rs_ready")
        attn_ready, vwin_mm, v2_ready = sem("attn_ready"), sem("vwin_mm"), sem("v2_ready")
        far_mm, farT_ready, bc_mm = sem("far_mm"), sem("farT_ready"), sem("bc_mm")
        bc_used, acc_added, bandT_mm = sem("bc_used"), sem("acc_added"), sem("bandT_mm")
        bandT_ready, pv_mm, o1_ready = sem("bandT_ready"), sem("pv_mm"), sem("o1_ready")
        ao_ready, out_mm, h2_ready = sem("ao_ready"), sem("out_mm"), sem("h2_ready")
        hc2_mm, sq2_ready, var2_mm = sem("hc2_mm"), sem("sq2_ready"), sem("var2_mm")
        lnv2_ready, rstd2_ready, x2_ready = sem("lnv2_ready"), sem("rstd2_ready"), sem("x2_ready")
        logit_mm, lg_ready, lmax_ready = sem("logit_mm"), sem("lg_ready"), sem("lmax_ready")
        m8_ready, i8_ready, idf_ready = sem("m8_ready"), sem("i8_ready"), sem("idf_ready")
        eq_ready, msk_ready, pos_mm = sem("eq_ready"), sem("msk_ready"), sem("pos_mm")
        lsub_ready, exr_ready, smr_ready = sem("lsub_ready"), sem("exr_ready"), sem("smr_ready")
        rcr_ready, kept_ready, room_ready = sem("rcr_ready"), sem("kept_ready"), sem("room_ready")
        kept2_ready, kw_ready, gs_ready = sem("kept2_ready"), sem("kw_ready"), sem("gs_ready")
        gt_ready, up_mm, gelu_ready = sem("gt_ready"), sem("up_mm"), sem("gelu_ready")
        down_mm, y1_ready, h2_turned = sem("down_mm"), sem("y1_ready"), sem("h2_turned")
        out_ready, band_in = sem("out_ready"), sem("band_in")
        scT_ready = sem("scT_ready")
        prod_ready = [sem(f"prod{c}_ready") for c in range(CH)]
        prod_used = [sem(f"prod{c}_used") for c in range(CH)]
        fprod_ready, fprod_used = sem("fprod_ready"), sem("fprod_used")
        x_in = [sem(f"x_in{s}") for s in range(2)]
        band_out = [sem(f"band_out{s}") for s in range(2)]
        out_stored = [sem(f"out_stored{s}") for s in range(2)]

        def after(eng, s, n):
            if isinstance(n, int) and n <= 0:
                return
            eng.wait_ge(s, n)

        def pipeline(eng, turn):
            def at(n):
                return Seq(n, n % 2, n // 2) if 0 <= n < BATCH else None
            turn(at(0), None, None, None)
            turn(at(1), at(0), None, None)
            turn(at(2), at(1), at(0), None)
            turn(at(3), at(2), at(1), at(0))
            with eng.Fori(0, (BATCH - 4) // 2) as i:
                for u in range(2):
                    turn(Seq(i * 2 + 4 + u, u, i + 2), Seq(i * 2 + 3 + u, 1 - u, i + 1 + u),
                         Seq(i * 2 + 2 + u, u, i + 1), Seq(i * 2 + 1 + u, 1 - u, i + u))
            turn(None, at(BATCH - 1), at(BATCH - 2), at(BATCH - 3))
            turn(None, None, at(BATCH - 1), at(BATCH - 2))
            turn(None, None, None, at(BATCH - 1))

        block = ctx.enter_context(nc.Block())

        @block.sync
        def _(sp):
            cut = COL["cen"][0]
            sp.dma_start(par[:, 0:cut], params[:, 0:cut]).then_inc(par_in, 16)
            sp.dma_start(par[:, cut:PCOLS], params[:, cut:PCOLS]).then_inc(par_in, 16)
            sp.dma_start(attn[0][:, :, :, :].rearrange("p t h o -> p (t h o)")[:, 0:ALLCOLS - PCOLS],
                         params[:, PCOLS:ALLCOLS]).then_inc(par_in, 16)

            def load_x(q_):
                after(sp, x_turned, q_.b - 1)
                sp.dma_start(xin[q_.s][:, :, :], x[q_.b, :, :].rearrange("(t p) d -> p t d", p=XT))\
                    .then_inc(x_in[q_.s], 16)

            def store_out(q_):
                sp.wait_ge(out_ready, TT * (q_.b + 1))
                full = 128 * (TT - 1)
                sp.dma_start(out[q_.b, 0:full, :].rearrange("(t p) d -> p t d", p=128),
                             osb[q_.s][:, 0:TT - 1, :]).then_inc(out_stored[q_.s], 16)
                sp.dma_start(out[q_.b, full:N, :], osb[q_.s][0:N - full, TT - 1, :]).then_inc(out_stored[q_.s], 16)

            def skew(q_):
                sp.wait_ge(attn_ready, q_.b + 1)
                n = 0
                while n < NP:
                    m = min(n // 128 * 128 + 128, n // BT * BT + BT)
                    t, p = n // 128, n % 128
                    dst = bass.AP(band_dram.tensor, q_.s * NP * HEADS * 128 + n * HEADS * 128 + n % BT,
                                  [[HEADS * 128 + 1, m - n], [128, HEADS], [1, DENSE]])
                    sp.dma_start(dst, attn[q_.s][p:p + m - n, t, :, 0:DENSE]).then_inc(band_out[q_.s], 16)
                    n = m
                after(sp, bandT_mm, 2 * NB * q_.b)
                sp.wait_ge(band_out[q_.s], 96 * (q_.g + 1))
                sp.dma_start(band[:, :, :], band_dram[q_.s, :, :].rearrange("(t p) w -> p t w", p=BT))\
                    .then_inc(band_in, 16)

            load_x(Seq(0, 0, 0))
            load_x(Seq(1, 1, 0))
            sp.wait_ge(pads_zero, 1)
            for s in range(2):
                for t in range(TT):
                    sp.dma_start(band_dram[s, 128 * t:128 * t + 128, :], v2[:, :, :, :].rearrange("p t h c -> p (t h c)")).then_inc(scratch_zero, 16)
            sp.wait_ge(scratch_zero, 16 * 2 * TT)

            def turn(T, S_, V, W):
                if T is not None and not (isinstance(T.b, int) and T.b < 2):
                    load_x(T)
                if W is not None:
                    store_out(W)
                if S_ is not None:
                    skew(S_)
            pipeline(sp, turn)
            sp.wait_ge(out_stored[0], 32 * BATCH // 2)
            sp.wait_ge(out_stored[1], 32 * BATCH // 2)

        @block.tensor
        def _(pe):
            mm, tr = nc.tensor.matmul, nc.tensor.transpose
            ident = P("ident")
            pe.wait_ge(par_in, 48)
            pe.wait_ge(setup_dve, 1)

            def project(q_):
                rhs = xn[q_.s][:, :]
                pe.wait_ge(xn_ready, q_.b + 1)
                mm(T1[:, 0:NP], P("qkv", 0, D), rhs, start=True, stop=True).then_inc(q_mm, 1)
                mm(T0[:, 0:NP], P("qkv", D, 2 * D), rhs, start=True, stop=True).then_inc(k_mm, 1)
                pe.wait_ge(q_ready, q_.b + 1)
                mm(T1[:, 0:NP], P("qkv", 2 * D, 3 * D), rhs, start=True, stop=True).then_inc(v_mm, 1)
                pe.wait_ge(k_ready, q_.b + 1)
                mm(T0[:, 0:NP], P("gatew"), rhs, start=True, stop=True).then_inc(gate_mm, 1)

            def convolve(q_):
                pe.wait_ge(x_in[q_.s], 16 * (q_.g + 1))
                after(pe, gate_ready, q_.b)
                for t in range(3):
                    last = tr(T0[:, t * XT:(t + 1) * XT], xin[q_.s][:, t, :], ident[0:XT, 0:XT])
                last.then_inc(x_turned, 1)
                pe.wait_ge(xT_ready, q_.b + 1)
                after(pe, v_ready, q_.b)
                for g, (dst, done) in enumerate(((T1, z_mm), (T0, f_mm), (T1, o_mm))):
                    if g == 2:
                        pe.wait_ge(z_ready, q_.b + 1)
                    mm(dst[:, 0:NP], P("conv", 2 * g * D, (2 * g + 1) * D), xT[:, 0:NP], start=True, stop=False)
                    mm(dst[:, 0:NP], P("conv", (2 * g + 1) * D, (2 * g + 2) * D), xT[:, 1:NP + 1],
                       start=False, stop=True).then_inc(done, 1)

            def center(q_):
                pe.wait_ge(f_ready, q_.b + 1)
                pe.wait_ge(h_ready, q_.b + 1)
                mm(T0[:, 0:NP], P("cen4"), h[q_.s][:, :], start=True, stop=True).then_inc(hc_mm, 1)

            def variance(q_):
                pe.wait_ge(o_ready, q_.b + 1)
                pe.wait_ge(sq_ready, q_.b + 1)
                mm(T1[:, 0:NP], P("avg"), sq[:, :], start=True, stop=True).then_inc(var_mm, 1)

            def score(q_, c):
                if c < CH:
                    src, ready, used, n = prod[c], prod_ready[c], prod_used[c], CW
                else:
                    src, ready, used, n = fprod, fprod_ready, fprod_used, LAST
                if c == 0:
                    after(pe, sc_ready, TT * q_.b)
                pe.wait_ge(ready, q_.b + 1)
                for r in range(4):
                    for g in range(4):
                        j = 4 * g + r
                        if j < n:
                            last = mm(S[c][32 * g:32 * g + 32, 0:N], ew[:, c * CW + j, :], src[:, j, :],
                                      start=(r == 0), stop=(r == min(3, n - 1 - 4 * g)))
                last.then_inc(used, 1)

            def turn_scores(q_):
                pe.wait_ge(scT_ready, (CH + 1) * (q_.b + 1))
                for t in range(TT):
                    for c in range(CH + 1):
                        rows = min(128, (NO - c * CW + 3) // 4 * 32)
                        last = tr(S[t][:, c * 128:c * 128 + rows], scT[0:rows, c, t * 128:(t + 1) * 128],
                                  ident[0:rows, 0:rows])
                    last.then_inc(scores_mm, 1)

            def turn_values(q_):
                pe.wait_ge(attn_ready, q_.b + 1)
                after(pe, room_ready, q_.b)
                after(pe, out_ready, TT * q_.b)
                for t in range(NB):
                    last = tr(V0[:, t * 128:(t + 1) * 128], vT[q_.s][:, t * BT:t * BT + 128], ident)
                last.then_inc(vwin_mm, 1)

            def far_weights(q_):
                for t in range(TT):
                    last = tr(V1[0:HEADS * NFAR, t * 128:(t + 1) * 128], attnf[q_.s][:, t, :], ident)
                last.then_inc(far_mm, 1)
                pe.wait_ge(v2_ready, q_.b + 1)
                pe.wait_ge(farT_ready, q_.b + 1)
                for i, o in enumerate(FAR):
                    if i >= 2:
                        pe.wait_ge(bc_used, NFAR * q_.b + i - 1)
                    mm((V0, V1)[i % 2][:, o:NP], P("pick", i * 128, (i + 1) * 128)[0:HEADS * NFAR, :],
                       farT[:, o:NP], start=True, stop=True).then_inc(bc_mm, 1)

            def attend(q_):
                pe.wait_ge(band_in, 16 * (q_.b + 1))
                groups = 2 * NB

                def turn_band(g):
                    t, half = divmod(g, 2)
                    if g < 2:
                        pe.wait_ge(bc_used, NFAR * q_.b + NFAR - 1 + g)
                    else:
                        pe.wait_ge(bandT_ready, groups * q_.b + g - 1)
                    for i in range(4):
                        col = (4 * half + (0, 2, 1, 3)[i]) * 128
                        last = tr((V0, V1)[g % 2][:, i * BT:(i + 1) * BT], band[:, t, col:col + 128],
                                  ident[0:BT, 0:BT])
                    last.then_inc(bandT_mm, 1)

                turn_band(0)
                after(pe, y1_ready, q_.b)
                for g in range(groups):
                    t, half = divmod(g, 2)
                    if g + 1 < groups:
                        turn_band(g + 1)
                    pe.wait_ge(bandT_ready, groups * q_.b + g + 1)
                    for i in range(4):
                        hh = 4 * half + (0, 2, 1, 3)[i]
                        rows = 32 * (hh // 2)
                        last = mm(V2[rows:rows + 32, t * BT:(t + 1) * BT], v2[:, t, hh, :],
                                  bandT[g % 2][:, i * BT:(i + 1) * BT], start=(hh % 2 == 0), stop=(hh % 2 == 1))
                    last.then_inc(pv_mm, 1)

            def out_project(q_):
                pe.wait_ge(ao_ready, q_.b + 1)
                mm(V0[:, 0:NP], P("outw"), ao[:, :], start=True, stop=True).then_inc(out_mm, 1)

            def center2(q_):
                pe.wait_ge(h2_ready, q_.b + 1)
                mm(V1[:, 0:NP], P("cen"), h2[:, :], start=True, stop=True).then_inc(hc2_mm, 1)

            def variance2(q_):
                pe.wait_ge(sq2_ready, q_.b + 1)
                mm(V0[:, 0:NP], P("avg"), sq2[:, :], start=True, stop=True).then_inc(var2_mm, 1)

            def ffn(q_):
                pe.wait_ge(x2_ready, q_.b + 1)
                for t in range(TT):
                    last = mm(V0[:, t * EXPERTS:(t + 1) * EXPERTS], x2[:, t * 128:(t + 1) * 128], P("router"),
                              start=True, stop=True)
                last.then_inc(logit_mm, 1)
                for f in range(FC):
                    if f == 1:
                        pe.wait_ge(lg_ready, q_.b + 1)
                    if f >= 2:
                        pe.wait_ge(gelu_ready, FC * q_.b + f - 1)
                    mm((V1, V0)[f % 2][:, 0:NP], P("up", f * 128, (f + 1) * 128), x2[:, :], start=True, stop=True)\
                        .then_inc(up_mm, 1)
                pe.wait_ge(gelu_ready, FC * q_.b + FC - 1)
                pe.wait_ge(msk_ready, q_.b + 1)
                for t in range(TT):
                    for u in range(t):
                        mm(V1[:, t * EXPERTS:(t + 1) * EXPERTS], onesb[:, :], msk[:, u, :], start=(u == 0), stop=False)
                    mm(V1[:, t * EXPERTS:(t + 1) * EXPERTS], beforeb[:, :], msk[:, t, :], start=(t == 0), stop=True)
                for t in range(TT):
                    rows = min(128, N - t * 128)
                    last = mm(V1[:, TT * EXPERTS:(TT + 1) * EXPERTS], onesb[0:rows, :], msk[0:rows, t, :],
                              start=(t == 0), stop=(t == TT - 1))
                last.then_inc(pos_mm, 1)
                pe.wait_ge(gelu_ready, FC * (q_.b + 1))
                for t in range(TT):
                    for f in range(FC):
                        last = mm(V2[:, t * D:(t + 1) * D], hid[:, f, t * 128:(t + 1) * 128],
                                  P("down", f * D, (f + 1) * D), start=(f == 0), stop=(f == FC - 1))
                last.then_inc(down_mm, 1)
                for t in range(TT):
                    last = tr(V0[:, t * 128:(t + 1) * 128], h2[:, t * 128:(t + 1) * 128], ident)
                last.then_inc(h2_turned, 1)

            def turn(T, S_, V, W):
                if S_:
                    project(S_)
                if T:
                    convolve(T)
                if S_:
                    score(S_, 0)
                if V:
                    turn_values(V)
                    far_weights(V)
                if T:
                    center(T)
                if S_:
                    score(S_, 1)
                if T:
                    variance(T)
                if V:
                    attend(V)
                    out_project(V)
                if S_:
                    score(S_, 2)
                if V:
                    center2(V)
                if S_:
                    turn_scores(S_)
                if V:
                    variance2(V)
                    ffn(V)
            pipeline(pe, turn)

        @block.scalar
        def _(act):
            A = nc.scalar.activation

            def bias(c):
                return P("bias", c, c + 1)
            act.wait_ge(par_in, 48)
            act.wait_ge(setup_dve, 1)
            act.wait_ge(pads_zero, 1)

            def projections(q_):
                act.wait_ge(q_mm, q_.b + 1)
                after(act, fprod_used, q_.b - 1)
                A(q[q_.s][:, :], T1[:, 0:NP], ACT.Identity, bias=bias(BQ)).then_inc(q_ready, 1)
                act.wait_ge(k_mm, q_.b + 1)
                A(k[q_.s][:, KPAD:KPAD + NP], T0[:, 0:NP], ACT.Identity, bias=bias(BK)).then_inc(k_ready, 1)
                act.wait_ge(v_mm, q_.b + 1)
                after(act, ao_ready, q_.b - 1)
                A(vT[q_.s][:, LOCAL:LOCAL + NP], T1[:, 0:NP], ACT.Identity, bias=bias(BV)).then_inc(v_ready, 1)
                act.wait_ge(gate_mm, q_.b + 1)
                A(gate[q_.s][:, :], T0[:, 0:NP], ACT.Tanh, bias=hbias[:, BG:BG + 1], scale=0.5)\
                    .then_inc(gate_ready, 1)

            def gates(q_):
                act.wait_ge(x_turned, q_.b + 1)
                after(act, o_mm, q_.b)
                A(xT[:, 0:ROWS], T0[:, 0:ROWS], ACT.Copy).then_inc(xT_ready, 1)
                act.wait_ge(z_mm, q_.b + 1)
                after(act, h_ready, q_.b)
                A(zt[:, :], T1[:, 0:NP], ACT.Tanh, bias=bias(BZ)).then_inc(z_ready, 1)
                act.wait_ge(f_mm, q_.b + 1)
                A(ft[:, :], T0[:, 0:NP], ACT.Tanh, bias=hbias[:, BF:BF + 1], scale=0.5).then_inc(f_ready, 1)
                act.wait_ge(o_mm, q_.b + 1)
                A(ot[:, :], T1[:, 0:NP], ACT.Tanh, bias=hbias[:, BO:BO + 1], scale=0.5).then_inc(o_ready, 1)

            def norm(src, var, hc_mm, sq_, sq_ready, var_mm, lnv_, lnv_ready, rstd_, rstd_ready, used, b):
                act.wait_ge(hc_mm, b + 1)
                after(act, var_mm, b)
                A(sq_[:, :], src[:, 0:NP], ACT.Square).then_inc(sq_ready, 1)
                act.wait_ge(var_mm, b + 1)
                A(lnv_[:, :], var[:, 0:NP], ACT.Ln, bias=epsc[:, 0:1]).then_inc(lnv_ready, 1)
                act.wait_ge(lnv_ready, b + 1)
                after(act, used, b)
                A(rstd_[:, :], lnv_[:, :], ACT.Exp, scale=-0.5).then_inc(rstd_ready, 1)

            def norm1(q_):
                norm(T0, T1, hc_mm, sq, sq_ready, var_mm, lnv, lnv_ready, rstd, rstd_ready, xn_ready, q_.b)

            def norm2(q_):
                norm(V1, V0, hc2_mm, sq2, sq2_ready, var2_mm, lnv2, lnv2_ready, rstd2, rstd2_ready,
                     x2_ready, q_.b)

            def softmax_exp(q_):
                act.wait_ge(sub_ready, q_.b + 1)
                after(act, attn_ready, q_.b)
                A(ex[:, :, :], sc[:, :, :], ACT.Exp).then_inc(ex_ready, 1)

            def score_copies(q_):
                for c in range(CH + 1):
                    act.wait_ge(prod_used[c] if c < CH else fprod_used, q_.b + 1)
                    after(act, scores_mm, TT * q_.b)
                    rows = min(128, (NO - c * CW + 3) // 4 * 32)
                    A(scT[0:rows, c, 0:N], S[c][0:rows, 0:N], ACT.Copy).then_inc(scT_ready, 1)

            def value_blocks(q_):
                act.wait_ge(vwin_mm, q_.b + 1)
                after(act, pv_mm, 2 * NB * q_.b)
                for t in range(NB):
                    dst = bass.AP(v2[:, :, :, :].tensor, t * HEADS * 32,
                                  [[NB * HEADS * 32, 128], [64, HEADS // 2], [32 + HD, 2], [1, HD]])
                    last = A(dst, V0[:, t * 128:(t + 1) * 128].rearrange("p (i e d) -> p i e d", e=2, d=HD), ACT.Copy)
                last.then_inc(v2_ready, 1)

            def far_copy(q_):
                act.wait_ge(far_mm, q_.b + 1)
                after(act, bc_mm, NFAR * q_.b)
                A(farT[:, :], V1[0:HEADS * NFAR, 0:NP], ACT.Copy).then_inc(farT_ready, 1)

            def band_copies(q_):
                for g in range(2 * NB):
                    act.wait_ge(bandT_mm, 2 * NB * q_.b + g + 1)
                    after(act, pv_mm, 2 * NB * q_.b + g - 1)
                    A(bandT[g % 2][:, :], (V0, V1)[g % 2][:, 0:4 * BT], ACT.Copy).then_inc(bandT_ready, 1)

            def router_exp(q_):
                act.wait_ge(lsub_ready, q_.b + 1)
                after(act, kw_ready, q_.b)
                A(exr[:, :, :], lsub[:, :, :], ACT.Exp).then_inc(exr_ready, 1)

            def gelus(q_):
                after(act, down_mm, q_.b)
                for f in range(FC):
                    act.wait_ge(up_mm, FC * q_.b + f + 1)
                    A(hid[:, f, :], (V1, V0)[f % 2][:, 0:NP], ACT.Gelu, bias=bias(B1 + f)).then_inc(gelu_ready, 1)

            def turn(T, S_, V, W):
                if T or S_:
                    act.preload_act_table_set("gelu_and_others")
                if S_:
                    projections(S_)
                if T:
                    gates(T)
                if T or S_ or V:
                    act.preload_act_table_set("natural_log_exp_and_others")
                if V:
                    value_blocks(V)
                    far_copy(V)
                if T:
                    norm1(T)
                if V:
                    band_copies(V)
                if S_:
                    score_copies(S_)
                if V:
                    norm2(V)
                if S_:
                    softmax_exp(S_)
                if V:
                    router_exp(V)
                    act.preload_act_table_set("gelu_and_others")
                    gelus(V)
            pipeline(act, turn)

        @block.vector
        def _(dve):
            v = nc.vector
            dve.wait_ge(par_in, 48)
            v.tensor_scalar(hbias[:, :], P("bias"), 0.5, None, ALU.mult)
            v.memset(epsc[:, :], EPS)
            v.memset(room[:, :], float(CAP))
            v.tensor_copy(beforeb[:, :], P("before"))
            v.tensor_copy(onesb[:, :], P("ones"))
            v.tensor_scalar(gain2[:, :], P("gain"), 0.5, None, ALU.mult)
            v.tensor_scalar(se1[:, :], P("se"), 1.0, HD ** -0.5, ALU.add, ALU.mult).then_inc(setup_lin, 1)
            dve.wait_ge(setup_lin, 1)
            for r in range(4):
                n = (NO - r + 3) // 4
                v.tensor_tensor(bass.AP(ew[:, :, :].tensor, r * 32, [[NO * 32, 128], [4 * 32, n], [1, 32]]),
                                bass.AP(se1[:, :].tensor, r, [[NO, 128], [4, n], [0, 32]]),
                                P("ind", r * 32, (r + 1) * 32).unsqueeze(1).broadcast_to([128, n, 32]), ALU.mult)
            oh = P("cosk").rearrange("p (h o) -> p h o", o=NO)
            v.tensor_tensor(bias_oh, oh, P("amp").unsqueeze(2).broadcast_to([128, HEADS, NO]), ALU.mult)\
                .then_inc(setup_lin, 1)
            dve.wait_ge(setup_lin, 2)
            v.tensor_tensor(bias_oh, bias_oh, P("pos").rearrange("p (h o) -> p h o", o=NO), ALU.add)\
                .then_inc(setup_lin, 1)
            dve.wait_ge(setup_lin, 3)
            for t in range(TT):
                last = v.tensor_tensor(bm[:, t, :, :], bias_oh,
                                       P("mask", t * NO, (t + 1) * NO).unsqueeze(1).broadcast_to([128, HEADS, NO]),
                                       ALU.add)
            last.then_inc(setup_dve, 1)
            dve.wait_ge(setup_dve, 1)
            dve.wait_ge(pads_zero, 1)

            def recur(q_):
                dve.wait_ge(z_ready, q_.b + 1)
                dve.wait_ge(f_ready, q_.b + 1)
                v.tensor_scalar(forget[:, :], ft[:, :], 0.5, 0.5, ALU.mult, ALU.add)
                v.scalar_tensor_tensor(mixin[:, :], ft[:, :], 1.0, zt[:, :], ALU.subtract, ALU.mult)\
                    .then_inc(mixin_ready, 1)
                dve.wait_ge(mixin_ready, q_.b + 1)
                v.tensor_tensor_scan(cell[:, :], forget[:, :], mixin[:, :], 0.0, ALU.mult, ALU.add)\
                    .then_inc(c_ready, 1)
                dve.wait_ge(c_ready, q_.b + 1)
                dve.wait_ge(o_ready, q_.b + 1)
                after(dve, hkeep_ready, q_.b - 1)
                v.scalar_tensor_tensor(h[q_.s][:, :], ot[:, :], 1.0, cell[:, :], ALU.add, ALU.mult)\
                    .then_inc(h_ready, 1)

            def norm1(q_):
                dve.wait_ge(rstd_ready, q_.b + 1)
                after(dve, gate_ready, q_.b - 1)
                v.tensor_tensor(xn[q_.s][:, :], T0[:, 0:NP], rstd[:, :], ALU.mult).then_inc(xn_ready, 1)

            def products(q_, c):
                if c == 0:
                    dve.wait_ge(k_ready, q_.b + 1)
                after(dve, prod_used[c], q_.b)
                back = bass.AP(k[q_.s][:, :].tensor, KPAD - LOCAL + c * CW, [[KPAD + NP, 128], [1, CW], [1, N]])
                v.tensor_tensor(prod[c][:, :, :], q[q_.s][:, 0:N].unsqueeze(1).broadcast_to([128, CW, N]), back,
                                ALU.mult).then_inc(prod_ready[c], 1)

            def softmax_in(q_):
                for t in range(TT):
                    dve.wait_ge(scores_mm, TT * q_.b + t + 1)
                    v.tensor_tensor(sc[:, t * HEADS:(t + 1) * HEADS, :],
                                    S[t][:, 0:SC].rearrange("p (o h) -> p h o", h=HEADS), bm[:, t, :, :],
                                    ALU.add).then_inc(sc_ready, 1)
                dve.wait_ge(sc_ready, TT * (q_.b + 1))
                v.tensor_reduce(mx[:, :], sc[:, :, :], AX.X, ALU.max).then_inc(mx_ready, 1)
                dve.wait_ge(mx_ready, q_.b + 1)
                v.tensor_tensor(sc[:, :, :], sc[:, :, :], mx[:, :].unsqueeze(2).broadcast_to([128, TT * HEADS, NO]),
                                ALU.subtract).then_inc(sub_ready, 1)

            def softmax_out(q_):
                dve.wait_ge(ex_ready, q_.b + 1)
                v.tensor_reduce(sm[:, :], ex[:, :, :], AX.X, ALU.add).then_inc(sm_ready, 1)
                dve.wait_ge(sm_ready, q_.b + 1)
                v.reciprocal(rs[:, :], sm[:, :]).then_inc(rc_ready, 1)
                dve.wait_ge(rc_ready, q_.b + 1)
                rs3 = rs[:, :].rearrange("p (t h) -> p t h", h=HEADS)
                v.tensor_tensor(rs3, rs3, gain2[:, :].unsqueeze(1).broadcast_to([128, TT, HEADS]), ALU.mult)\
                    .then_inc(rs_ready, 1)
                dve.wait_ge(rs_ready, q_.b + 1)
                after(dve, band_out[q_.s], 96 * q_.g)
                after(dve, farT_ready, q_.b - 1)
                v.tensor_tensor(attn[q_.s][:, :, :, :].rearrange("p t h o -> p (t h) o"), ex[:, :, 0:DENSE],
                                rs[:, :].unsqueeze(2).broadcast_to([128, TT * HEADS, DENSE]), ALU.mult)
                v.tensor_tensor(attnf[q_.s][:, :, :].rearrange("p t (h o) -> p (t h) o", o=NFAR), ex[:, :, DENSE:NO],
                                rs[:, :].unsqueeze(2).broadcast_to([128, TT * HEADS, NFAR]), ALU.mult)\
                    .then_inc(attn_ready, 1)

            def far_values(q_):
                for i, o in enumerate(FAR):
                    dve.wait_ge(bc_mm, NFAR * q_.b + i + 1)
                    if 1 <= i:
                        after(dve, acc_added, (NFAR - 1) * q_.b + (i - 2 if i > 2 else 0))
                    dst = acc if i == 0 else tmp[i % 2]
                    v.tensor_tensor(dst[:, o:NP], (V0, V1)[i % 2][:, o:NP], vT[q_.s][:, LOCAL:LOCAL + NP - o],
                                    ALU.mult).then_inc(bc_used, 1)

            def attention_out(q_):
                dve.wait_ge(pv_mm, 2 * NB * (q_.b + 1))
                dve.wait_ge(acc_added, (NFAR - 1) * (q_.b + 1))
                v.tensor_tensor(o1[:, :], V2[:, 0:NP], acc[:, :], ALU.add).then_inc(o1_ready, 1)
                dve.wait_ge(o1_ready, q_.b + 1)
                v.scalar_tensor_tensor(ao[:, :], gate[q_.s][:, :], 1.0, o1[:, :], ALU.add, ALU.mult)\
                    .then_inc(ao_ready, 1)

            def residual(q_):
                dve.wait_ge(out_mm, q_.b + 1)
                dve.wait_ge(hkeep_ready, q_.b + 1)
                v.scalar_tensor_tensor(h2[:, :], V0[:, 0:NP], P("bias", BOUT, BOUT + 1), hkeep[q_.s][:, :],
                                       ALU.add, ALU.add).then_inc(h2_ready, 1)

            def norm2(q_):
                dve.wait_ge(rstd2_ready, q_.b + 1)
                v.tensor_tensor(x2[:, :], V1[:, 0:NP], rstd2[:, :], ALU.mult).then_inc(x2_ready, 1)

            def route(q_):
                dve.wait_ge(logit_mm, q_.b + 1)
                v.tensor_copy(lg[:, :, :], V0[:, 0:TT * EXPERTS].rearrange("p (t e) -> p t e", e=EXPERTS))\
                    .then_inc(lg_ready, 1)
                dve.wait_ge(lg_ready, q_.b + 1)
                v.tensor_reduce(lmax[:, :], lg[:, :, :], AX.X, ALU.max).then_inc(lmax_ready, 1)
                for t in range(TT):
                    last = v.max(m8[:, t, :], lg[:, t, :])
                last.then_inc(m8_ready, 1)
                dve.wait_ge(lmax_ready, q_.b + 1)
                dve.wait_ge(m8_ready, q_.b + 1)
                v.tensor_tensor(lsub[:, :, :], lg[:, :, :], lmax[:, :].unsqueeze(2).broadcast_to([128, TT, EXPERTS]),
                                ALU.subtract).then_inc(lsub_ready, 1)
                for t in range(TT):
                    last = v.max_index(i8[:, t, :], m8[:, t, :], lg[:, t, :])
                last.then_inc(i8_ready, 1)
                dve.wait_ge(i8_ready, q_.b + 1)
                v.tensor_copy(idf[:, :, :], i8[:, :, 0:TOPK]).then_inc(idf_ready, 1)
                dve.wait_ge(idf_ready, q_.b + 1)
                iota = P("iota").unsqueeze(1).broadcast_to([128, TT, EXPERTS])
                v.tensor_tensor(eq0[:, :, :], iota, idf[:, :, 0:1].broadcast_to([128, TT, EXPERTS]), ALU.is_equal)
                v.tensor_tensor(eq1[:, :, :], iota, idf[:, :, 1:2].broadcast_to([128, TT, EXPERTS]), ALU.is_equal)\
                    .then_inc(eq_ready, 1)
                dve.wait_ge(eq_ready, q_.b + 1)
                v.tensor_tensor(msk[:, :, :], eq0[:, :, :], eq1[:, :, :], ALU.add).then_inc(msk_ready, 1)

            def weigh(q_):
                dve.wait_ge(pos_mm, q_.b + 1)
                v.tensor_tensor(kept[:, :, :], V1[:, 0:TT * EXPERTS].rearrange("p (t e) -> p t e", e=EXPERTS),
                                room[:, :].unsqueeze(1).broadcast_to([128, TT, EXPERTS]), ALU.is_lt)\
                    .then_inc(kept_ready, 1)
                dve.wait_ge(kept_ready, q_.b + 1)
                v.tensor_tensor(room[:, :], room[:, :], V1[:, TT * EXPERTS:(TT + 1) * EXPERTS], ALU.subtract)\
                    .then_inc(room_ready, 1)
                v.tensor_tensor(kept[:, :, :], kept[:, :, :], msk[:, :, :], ALU.mult).then_inc(kept2_ready, 1)
                dve.wait_ge(kept2_ready, q_.b + 1)
                dve.wait_ge(exr_ready, q_.b + 1)
                v.tensor_tensor(kw[:, :, :], kept[:, :, :], exr[:, :, :], ALU.mult)
                v.tensor_reduce(smr[:, :], exr[:, :, :], AX.X, ALU.add).then_inc(kw_ready, 1)
                dve.wait_ge(kw_ready, q_.b + 1)
                v.tensor_reduce(gs[:, :], kw[:, :, :], AX.X, ALU.add)
                v.reciprocal(rcr[:, :], smr[:, :]).then_inc(gs_ready, 1)
                dve.wait_ge(gs_ready, q_.b + 1)
                v.tensor_tensor(gt[:, :], gs[:, :], rcr[:, :], ALU.mult).then_inc(gt_ready, 1)

            def finish(q_):
                dve.wait_ge(down_mm, q_.b + 1)
                v.tensor_tensor(y1[:, :, :], V2[:, 0:TT * D].rearrange("p (t d) -> p t d", d=D),
                                P("b2").unsqueeze(1).broadcast_to([128, TT, D]), ALU.add).then_inc(y1_ready, 1)
                dve.wait_ge(y1_ready, q_.b + 1)
                dve.wait_ge(gt_ready, q_.b + 1)
                dve.wait_ge(h2_turned, q_.b + 1)
                after(dve, out_stored[q_.s], 32 * q_.g)
                for t in range(TT):
                    v.scalar_tensor_tensor(osb[q_.s][:, t, :], y1[:, t, :], gt[:, t:t + 1],
                                           V0[:, t * D:(t + 1) * D], ALU.mult, ALU.add).then_inc(out_ready, 1)

            def turn(T, S_, V, W):
                if S_:
                    products(S_, 0)
                if T:
                    recur(T)
                if S_:
                    products(S_, 1)
                if V:
                    far_values(V)
                if T:
                    norm1(T)
                if V:
                    attention_out(V)
                    residual(V)
                if S_:
                    softmax_in(S_)
                if V:
                    norm2(V)
                    route(V)
                if S_:
                    softmax_out(S_)
                if V:
                    weigh(V)
                    finish(V)
            pipeline(dve, turn)

        @block.gpsimd
        def _(pool):
            g = nc.gpsimd
            g.memset(xT[:, ROWS:NP + 1], 0.0)
            g.memset(back4[:, :], -0.25)
            for s in range(2):
                g.memset(k[s][:, 0:KPAD], 0.0)
                g.memset(vT[s][:, 0:LOCAL], 0.0)
            g.memset(scT[:, :, N:NP], 0.0)
            g.memset(fprod[:, :, :], 0.0)
            g.memset(acc[:, 0:FAR[0]], 0.0)
            g.memset(v2[:, :, :, :], 0.0).then_inc(pads_zero, 1)
            pool.wait_ge(pads_zero, 1)

            def carry(q_):
                pool.wait_ge(h_ready, q_.b + 1)
                after(pool, h2_ready, q_.b - 1)
                g.tensor_tensor(hkeep[q_.s][:, :], h[q_.s][:, :], back4[:, :].broadcast_to([128, NP]), ALU.mult)\
                    .then_inc(hkeep_ready, 1)

            def far_products(q_):
                pool.wait_ge(k_ready, q_.b + 1)
                after(pool, fprod_used, q_.b)
                for i, o in enumerate(OFFS[CH * CW:]):
                    last = g.tensor_tensor(fprod[:, i, o:N], q[q_.s][:, o:N], k[q_.s][:, KPAD:KPAD + N - o], ALU.mult)
                last.then_inc(fprod_ready, 1)

            def far_sum(q_):
                for i in range(1, NFAR):
                    o = FAR[i]
                    pool.wait_ge(bc_used, NFAR * q_.b + i + 1)
                    after(pool, acc_added, (NFAR - 1) * q_.b + i - 1)
                    g.tensor_tensor(acc[:, o:NP], acc[:, o:NP], tmp[i % 2][:, o:NP], ALU.add).then_inc(acc_added, 1)

            def turn(T, S_, V, W):
                if S_:
                    carry(S_)
                if S_:
                    far_products(S_)
                if V:
                    far_sum(V)
            pipeline(pool, turn)


def _params(i):
    f = np.float32
    a = {}
    a["ident"] = np.eye(128, dtype=f)
    a["conv"] = np.concatenate([i["L0_tok_W_" + g][:, :, t].T for g in "zfo" for t in range(2)], axis=1)
    cols = [i["L0_tok_b_" + g][:, None] for g in "zfo"]
    qb = i["L0_attn_b_qkv"]
    cols += [qb[D * t:D * (t + 1), None] for t in range(3)]
    cols += [i["L0_attn_b_gate"][:, None], i["L0_attn_b_out"][:, None], i["L0_ffn_b1"].reshape(FC, 128).T]
    a["bias"] = np.concatenate(cols, axis=1)
    a["cen"] = (np.eye(128) - 1.0 / 128).astype(f)
    a["cen4"] = a["cen"] * f(-0.25)
    a["avg"] = np.full((128, 128), 1.0 / 128, f)
    a["qkv"] = i["L0_attn_W_qkv"]
    a["gatew"] = i["L0_attn_W_gate"]
    order = OFFS_INDEX
    a["se"] = np.tile(i["L0_attn_scale_embed"][order].T, (HEADS, 1))
    ch = np.arange(128)
    col = np.arange(32)[None, None, :]
    a["ind"] = (col == 8 * np.arange(4)[None, :, None] + ch[:, None, None] // HD).astype(f).reshape(128, 128)
    a["pos"] = np.broadcast_to(i["L0_attn_pos_bias"][order].T.reshape(1, SC), (128, SC))
    log_max = np.log(1.0 + 4096.0)
    om = np.array([0.0, 0.0, 1, 1, 4, 4, 6, 6]) * np.pi / log_max
    logd = np.log(1.0 + np.array(OFFS, np.float64))
    cosk = np.where(om[:, None] > 0, np.cos(om[:, None] * logd[None, :]), 0.0).astype(f)
    a["cosk"] = np.broadcast_to(cosk.reshape(1, SC), (128, SC))
    a["amp"] = np.broadcast_to(i["L0_attn_disp_amp"][None, :], (128, HEADS))
    a["gain"] = np.broadcast_to(i["L0_attn_if_gain"][None, :], (128, HEADS))
    tok = ch[:, None, None] + 128 * np.arange(TT)[None, :, None]
    a["mask"] = np.where(tok >= np.array(OFFS)[None, None, :], 0.0, MASKED).astype(f).reshape(128, TT * NO)
    pick = np.zeros((128, NFAR, 128), f)
    for hh in range(HEADS):
        for s in range(NFAR):
            pick[hh * NFAR + s, s, hh * HD:(hh + 1) * HD] = 1.0
    a["pick"] = pick.reshape(128, NFAR * 128)
    a["outw"] = i["L0_attn_W_out"]
    a["router"] = i["L0_ffn_router_w"].T
    a["up"] = i["L0_ffn_w1"].T
    a["down"] = i["L0_ffn_w2"].T.reshape(FC, 128, D).transpose(1, 0, 2).reshape(128, FC * D)
    a["b2"] = np.broadcast_to(i["L0_ffn_b2"][None, :], (128, D))
    a["iota"] = np.broadcast_to(np.arange(EXPERTS, dtype=f)[None, :], (128, EXPERTS))
    a["before"] = (ch[:, None] < ch[None, :]).astype(f)
    a["ones"] = np.ones((128, 128), f)
    for n, w in FIELDS + SETUP:
        assert a[n].shape == (128, w), (n, a[n].shape)
    return np.ascontiguousarray(np.concatenate([a[n] for n, _ in FIELDS + SETUP], axis=1))


OFFS_INDEX = [LOCAL - j for j in range(DENSE)] + [DENSE + s for s in range(NFAR)]


def kernel(**inputs):
    import concourse.bacc as _bacc
    from concourse.bass_utils import run_bass_kernel_spmd as _run

    i = {n: np.asarray(a) for n, a in inputs.items()}
    arrays = {"x_dram": np.ascontiguousarray(i["x"]), "params_dram": _params(i)}
    nc = _bacc.Bacc("TRN2", target_bir_lowering=False, num_devices=1)
    f32 = mybir.dt.float32
    x = nc.dram_tensor("x_dram", [BATCH, ROWS, D], f32, kind="ExternalInput").ap()
    params = nc.dram_tensor("params_dram", [128, ALLCOLS], f32, kind="ExternalInput").ap()
    out = nc.dram_tensor("out_dram", [BATCH, N, D], f32, kind="ExternalOutput").ap()
    build(nc, x, params, out)
    r = _run(nc, [arrays], core_ids=[0])
    return r.results[0]["out_dram"]
```

```python
import numpy as np
import concourse.bass as bass
from concourse import mybir
from contextlib import ExitStack

BATCH, ROWS, D = 16, 375, 128
N = ROWS - 1
NP = 384
TT = NP // 128
BT, NB = 96, NP // 96
HEADS, HD = 8, 16
LOCAL = 32
DENSE = LOCAL + 1
FAR = [48, 64, 96, 128, 192, 256]
NFAR = len(FAR)
OFFS = [LOCAL - j for j in range(DENSE)] + FAR
NO = len(OFFS)
CW = 16
CH = NO // CW
PARTS = 4
LAST = NO - CH * CW
KPAD = max(FAR)
SC = HEADS * NO
EXPERTS, TOPK, CAP, FFN = 64, 2, 128, 512
FC = FFN // 128
EPS = 1e-5
MASKED = -1e30
XT = 125

FIELDS = [
    ("ident", 128), ("conv", 6 * D), ("bias", 12), ("cen", 128), ("cen4", 128), ("avg", 128),
    ("qkv", 3 * D), ("gatew", D),
    ("se", NO), ("ind", 4 * 32), ("amp", HEADS), ("gain", HEADS), ("pick", NFAR * 128), ("outw", D), ("router", EXPERTS), ("up", FFN), ("down", FC * D), ("b2", D),
    ("iota", EXPERTS), ("before", 128), ("ones", 128),
]
SETUP = [("pos", SC), ("cosk", SC), ("mask", TT * NO)]
COL, _at = {}, 0
for _n, _w in FIELDS:
    COL[_n] = (_at, _at + _w)
    _at += _w
PCOLS = _at
for _n, _w in SETUP:
    COL[_n] = (_at, _at + _w)
    _at += _w
ALLCOLS = _at
BZ, BF, BO, BQ, BK, BV, BG, BOUT, B1 = 0, 1, 2, 3, 4, 5, 6, 7, 8


class Seq:

    def __init__(self, b, s, g):
        self.b, self.s, self.g = b, s, g


def build(nc, x, params, out):
    fp32, bf16, u32 = mybir.dt.float32, mybir.dt.bfloat16, mybir.dt.uint32
    ALU, ACT, AX = mybir.AluOpType, mybir.ActivationFunctionType, mybir.AxisListType
    band_dram = nc.dram_tensor("band_scratch", [2, NP, HEADS * 128], fp32, kind="Internal").ap()

    with ExitStack() as ctx:
        def sb(name, shape, dt=fp32):
            return ctx.enter_context(nc.sbuf_tensor(name, shape, dt))

        def bank(name):
            return ctx.enter_context(nc.psum_tensor(name, [128, 512], fp32))

        def sem(name):
            return ctx.enter_context(nc.semaphore(name))

        par = sb("par", [128, PCOLS])

        def P(name, a=0, b=None):
            lo, hi = COL[name]
            if lo >= PCOLS:
                flat = attn[0][:, :, :, :].rearrange("p t h o -> p (t h o)")
                return flat[:, lo - PCOLS + a:(hi if b is None else lo + b) - PCOLS]
            return par[:, lo + a:(hi if b is None else lo + b)]

        xin = [sb(f"xin{s}", [XT, 3, D]) for s in range(2)]
        xT = sb("xT", [128, NP + 1])
        zt, ft, ot = sb("zt", [128, NP]), sb("ft", [128, NP]), sb("ot", [128, NP])
        forget, mixin, cell = sb("forget", [128, NP]), sb("mixin", [128, NP]), sb("cell", [128, NP])
        back4 = sb("back4", [128, 1])
        h = [sb(f"h{s}", [128, NP]) for s in range(2)]
        hkeep = [sb(f"hkeep{s}", [128, NP]) for s in range(2)]
        stat = sb("stat", [128, NP])
        xn = [sb(f"xn{s}", [128, NP]) for s in range(2)]
        q = [sb(f"q{s}", [128, NP]) for s in range(2)]
        k = [sb(f"k{s}", [128, KPAD + NP]) for s in range(2)]
        vT = [sb(f"vT{s}", [128, LOCAL + NP]) for s in range(2)]
        gate = [sb(f"gate{s}", [128, NP]) for s in range(2)]
        prod = [sb(f"prod{c}", [128, CW, N]) for c in range(CH)]
        fprod = sb("fprod", [128, LAST, N])
        ew = sb("ew", [128, NO, 32])
        scT = sb("scT", [128, CH + 1, NP])
        bm = sb("bm", [128, TT, HEADS, NO])
        sc = sb("sc", [128, TT * HEADS, NO])
        ex = sb("ex", [128, TT * HEADS, NO])
        mx, sm, rs = sb("mx", [128, TT * HEADS]), sb("sm", [128, TT * HEADS]), sb("rs", [128, TT * HEADS])
        attn = [sb(f"attn{s}", [128, TT, HEADS, DENSE]) for s in range(2)]
        attnf = [sb(f"attnf{s}", [128, TT, HEADS * NFAR]) for s in range(2)]
        band = sb("band", [BT, NB, HEADS * 128])
        bandT = [sb(f"bandT{i}", [128, 4 * BT]) for i in range(2)]
        v2 = sb("v2", [128, NB, HEADS, 32])
        farT = sb("farT", [HEADS * NFAR, NP])
        acc = sb("acc", [128, NP])
        tmp = [sb(f"tmp{i}", [128, NP]) for i in range(2)]
        o1, ao = sb("o1", [128, NP]), sb("ao", [128, NP])
        h2 = [sb(f"h2{s}", [128, NP]) for s in range(2)]
        stat2, x2 = sb("stat2", [128, NP]), sb("x2", [128, NP])
        lg, lsub, exr = (sb(n, [128, TT, EXPERTS]) for n in ("lg", "lsub", "exr"))
        m8 = sb("m8", [128, TT, 8])
        i8 = sb("i8", [128, TT, 8], u32)
        idf = sb("idf", [128, TT, TOPK])
        eq0, eq1 = sb("eq0", [128, TT, EXPERTS]), sb("eq1", [128, TT, EXPERTS])
        msk = sb("msk", [128, TT, EXPERTS], bf16)
        room = sb("room", [128, EXPERTS])
        kept, kw = sb("kept", [128, TT, EXPERTS]), sb("kw", [128, TT, EXPERTS])
        lmax, gs, smr, rcr, gt = (sb(n, [128, TT]) for n in ("lmax", "gs", "smr", "rcr", "gt"))
        beforeb, onesb = sb("beforeb", [128, 128], bf16), sb("onesb", [128, 128], bf16)
        hid = sb("hid", [128, FC, NP])
        y1 = sb("y1", [128, TT, D])
        osb = [sb(f"osb{s}", [128, TT, D]) for s in range(2)]
        hbias = sb("hbias", [128, 12])
        epsc = sb("epsc", [128, 1])
        se1 = sb("se1", [128, NO])
        gain2 = sb("gain2", [128, HEADS])
        bias_oh = attn[1][:, :, :, :].rearrange("p t h o -> p (t h o)")[:, 0:SC].rearrange("p (h o) -> p h o", o=NO)

        T0, T1 = bank("T0"), bank("T1")
        S = [bank(f"S{t}") for t in range(TT)]
        V0, V1, V2 = bank("V0"), bank("V1"), bank("V2")

        par_in, pads_zero, scratch_zero = sem("par_in"), sem("pads_zero"), sem("scratch_zero")
        setup_dve, setup_lin, x_turned = sem("setup_dve"), sem("setup_lin"), sem("x_turned")
        xT_ready, z_mm, z_ready = sem("xT_ready"), sem("z_mm"), sem("z_ready")
        f_mm, f_ready, o_mm = sem("f_mm"), sem("f_ready"), sem("o_mm")
        o_ready, mixin_ready, c_ready = sem("o_ready"), sem("mixin_ready"), sem("c_ready")
        h_ready, hc_mm, sq_ready = sem("h_ready"), sem("hc_mm"), sem("sq_ready")
        var_mm, lnv_ready, rstd_ready = sem("var_mm"), sem("lnv_ready"), sem("rstd_ready")
        xn_ready, q_mm, q_ready = sem("xn_ready"), sem("q_mm"), sem("q_ready")
        k_mm, k_ready, v_mm = sem("k_mm"), sem("k_ready"), sem("v_mm")
        v_ready, gate_mm, gate_ready = sem("v_ready"), sem("gate_mm"), sem("gate_ready")
        hkeep_ready, scores_mm, sc_ready = sem("hkeep_ready"), sem("scores_mm"), sem("sc_ready")
        mx_ready, sub_ready, ex_ready = sem("mx_ready"), sem("sub_ready"), sem("ex_ready")
        sm_ready, rc_ready, rs_ready = sem("sm_ready"), sem("rc_ready"), sem("rs_ready")
        attn_ready, vwin_mm, v2_ready = sem("attn_ready"), sem("vwin_mm"), sem("v2_ready")
        far_mm, farT_ready, bc_mm = sem("far_mm"), sem("farT_ready"), sem("bc_mm")
        bc_used, acc_added, bandT_mm = sem("bc_used"), sem("acc_added"), sem("bandT_mm")
        bandT_ready, pv_mm, o1_ready = sem("bandT_ready"), sem("pv_mm"), sem("o1_ready")
        ao_ready, out_mm, h2_ready = sem("ao_ready"), sem("out_mm"), sem("h2_ready")
        hc2_mm, sq2_ready, var2_mm = sem("hc2_mm"), sem("sq2_ready"), sem("var2_mm")
        lnv2_ready, rstd2_ready, x2_ready = sem("lnv2_ready"), sem("rstd2_ready"), sem("x2_ready")
        logit_mm, lg_ready, lmax_ready = sem("logit_mm"), sem("lg_ready"), sem("lmax_ready")
        m8_ready, i8_ready, idf_ready = sem("m8_ready"), sem("i8_ready"), sem("idf_ready")
        eq_ready, msk_ready, pos_mm = sem("eq_ready"), sem("msk_ready"), sem("pos_mm")
        lsub_ready, exr_ready, smr_ready = sem("lsub_ready"), sem("exr_ready"), sem("smr_ready")
        rcr_ready, kept_ready, room_ready = sem("rcr_ready"), sem("kept_ready"), sem("room_ready")
        kept2_ready, kw_ready, gs_ready = sem("kept2_ready"), sem("kw_ready"), sem("gs_ready")
        gt_ready, up_mm, gelu_ready = sem("gt_ready"), sem("up_mm"), sem("gelu_ready")
        down_mm, y1_ready, h2_turned = sem("down_mm"), sem("y1_ready"), sem("h2_turned")
        out_ready, band_in = sem("out_ready"), sem("band_in")
        scT_ready = sem("scT_ready")
        prod_ready = [sem(f"prod{c}_ready") for c in range(CH)]
        prod_used = [sem(f"prod{c}_used") for c in range(CH)]
        fprod_ready, fprod_used = sem("fprod_ready"), sem("fprod_used")
        x_in = [sem(f"x_in{s}") for s in range(2)]
        band_out = [sem(f"band_out{s}") for s in range(2)]
        out_stored = [sem(f"out_stored{s}") for s in range(2)]

        def after(eng, s, n):
            if isinstance(n, int) and n <= 0:
                return
            eng.wait_ge(s, n)

        def pipeline(eng, turn, lags=(0, 1, 2, 3)):
            def at(n):
                return Seq(n, n % 2, n // 2) if 0 <= n < BATCH else None
            for n in range(4):
                turn(*(at(n - lag) for lag in lags))
            with eng.Fori(0, (BATCH - 4) // 2) as i:
                for u in range(4, 6):
                    turn(*(Seq(i * 2 + u - lag, (u - lag) % 2, i + (u - lag) // 2) for lag in lags))
            for n in range(BATCH, BATCH + max(lags)):
                turn(*(at(n - lag) for lag in lags))

        block = ctx.enter_context(nc.Block())

        @block.sync
        def _(sp):
            cut = COL["cen"][0]
            sp.dma_start(par[:, 0:cut], params[:, 0:cut]).then_inc(par_in, 16)
            sp.dma_start(par[:, cut:PCOLS], params[:, cut:PCOLS]).then_inc(par_in, 16)
            sp.dma_start(attn[0][:, :, :, :].rearrange("p t h o -> p (t h o)")[:, 0:ALLCOLS - PCOLS],
                         params[:, PCOLS:ALLCOLS]).then_inc(par_in, 16)

            def load_x(q_):
                after(sp, x_turned, q_.b - 1)
                sp.dma_start(xin[q_.s][:, :, :], x[q_.b, :, :].rearrange("(t p) d -> p t d", p=XT))\
                    .then_inc(x_in[q_.s], 16)

            def store_out(q_):
                sp.wait_ge(out_ready, TT * (q_.b + 1))
                full = 128 * (TT - 1)
                sp.dma_start(out[q_.b, 0:full, :].rearrange("(t p) d -> p t d", p=128),
                             osb[q_.s][:, 0:TT - 1, :]).then_inc(out_stored[q_.s], 16)
                sp.dma_start(out[q_.b, full:N, :], osb[q_.s][0:N - full, TT - 1, :]).then_inc(out_stored[q_.s], 16)

            def skew(q_):
                sp.wait_ge(attn_ready, q_.b + 1)
                n = 0
                while n < NP:
                    m = min(n // 128 * 128 + 128, n // BT * BT + BT)
                    t, p = n // 128, n % 128
                    dst = bass.AP(band_dram.tensor, q_.s * NP * HEADS * 128 + n * HEADS * 128 + n % BT,
                                  [[HEADS * 128 + 1, m - n], [128, HEADS], [1, DENSE]])
                    sp.dma_start(dst, attn[q_.s][p:p + m - n, t, :, 0:DENSE]).then_inc(band_out[q_.s], 16)
                    n = m
                after(sp, bandT_mm, 2 * NB * q_.b)
                sp.wait_ge(band_out[q_.s], 96 * (q_.g + 1))
                sp.dma_start(band[:, :, :], band_dram[q_.s, :, :].rearrange("(t p) w -> p t w", p=BT))\
                    .then_inc(band_in, 16)

            load_x(Seq(0, 0, 0))
            sp.wait_ge(pads_zero, 1)
            for s in range(2):
                for t in range(TT):
                    sp.dma_start(band_dram[s, 128 * t:128 * t + 128, :], v2[:, :, :, :].rearrange("p t h c -> p (t h c)")).then_inc(scratch_zero, 16)
            sp.wait_ge(scratch_zero, 16 * 2 * TT)

            def turn(T, S_, W):
                if T is not None and not (isinstance(T.b, int) and T.b < 1):
                    load_x(T)
                if S_ is not None:
                    skew(S_)
                if W is not None:
                    store_out(W)
            pipeline(sp, turn, lags=(0, 2, 4))
            sp.wait_ge(out_stored[0], 32 * BATCH // 2)
            sp.wait_ge(out_stored[1], 32 * BATCH // 2)

        @block.tensor
        def _(pe):
            mm, tr = nc.tensor.matmul, nc.tensor.transpose
            ident = P("ident")
            pe.wait_ge(par_in, 48)
            pe.wait_ge(setup_dve, 1)

            def project_qk(q_):
                pe.wait_ge(xn_ready, q_.b + 1)
                mm(T1[:, 0:NP], P("qkv", 0, D), xn[q_.s][:, :], start=True, stop=True).then_inc(q_mm, 1)
                mm(T0[:, 0:NP], P("qkv", D, 2 * D), xn[q_.s][:, :], start=True, stop=True).then_inc(k_mm, 1)

            def project_v(q_):
                pe.wait_ge(q_ready, q_.b + 1)
                mm(T1[:, 0:NP], P("qkv", 2 * D, 3 * D), xn[q_.s][:, :], start=True, stop=True).then_inc(v_mm, 1)

            def project_gate(q_):
                pe.wait_ge(v_ready, q_.b + 1)
                mm(T1[:, 0:NP], P("gatew"), xn[q_.s][:, :], start=True, stop=True).then_inc(gate_mm, 1)

            def turn_x(q_):
                pe.wait_ge(x_in[q_.s], 16 * (q_.g + 1))
                after(pe, k_ready, q_.b)
                for t in range(3):
                    last = tr(T0[:, t * XT:(t + 1) * XT], xin[q_.s][:, t, :], ident[0:XT, 0:XT])
                last.then_inc(x_turned, 1)

            def convolve(q_, g):
                pe.wait_ge((xT_ready, z_ready, f_ready)[g], q_.b + 1)
                mm(T0[:, 0:NP], P("conv", 2 * g * D, (2 * g + 1) * D), xT[:, 0:NP], start=True, stop=False)
                mm(T0[:, 0:NP], P("conv", (2 * g + 1) * D, (2 * g + 2) * D), xT[:, 1:NP + 1],
                   start=False, stop=True).then_inc((z_mm, f_mm, o_mm)[g], 1)

            def center(q_, F):
                if F:
                    pe.wait_ge(gelu_ready, FC * (F.b + 1))
                pe.wait_ge(h_ready, q_.b + 1)
                mm(T0[:, 0:NP], P("cen4"), h[q_.s][:, :], start=True, stop=True).then_inc(hc_mm, 1)

            def variance(q_, S_):
                if S_:
                    pe.wait_ge(gate_ready, S_.b + 1)
                pe.wait_ge(sq_ready, q_.b + 1)
                mm(T1[:, 0:NP], P("avg"), stat[:, :], start=True, stop=True).then_inc(var_mm, 1)

            def score(q_, c, steps=range(4)):
                if c < CH:
                    src, ready, used, n = prod[c], prod_ready[c], prod_used[c], CW
                else:
                    src, ready, used, n = fprod, fprod_ready, fprod_used, LAST
                if c == 0:
                    after(pe, sc_ready, TT * q_.b)
                if c == CH:
                    pe.wait_ge(ready, q_.b + 1)
                for r in steps:
                    if c < CH:
                        pe.wait_ge(ready, PARTS * q_.b + r + 1)
                    for g in range(4):
                        j = 4 * g + r
                        if j < n:
                            last = mm(S[c][32 * g:32 * g + 32, 0:N], ew[:, c * CW + j, :], src[:, j, :],
                                      start=(r == 0), stop=(r == min(3, n - 1 - 4 * g)))
                if 3 in steps:
                    last.then_inc(used, 1)

            def turn_scores(q_):
                pe.wait_ge(scT_ready, (CH + 1) * (q_.b + 1))
                for t in range(TT):
                    for c in range(CH + 1):
                        rows = min(128, (NO - c * CW + 3) // 4 * 32)
                        last = tr(S[t][:, c * 128:c * 128 + rows], scT[0:rows, c, t * 128:(t + 1) * 128],
                                  ident[0:rows, 0:rows])
                    last.then_inc(scores_mm, 1)

            def turn_values(q_):
                pe.wait_ge(attn_ready, q_.b + 1)
                after(pe, x2_ready, q_.b)
                after(pe, out_ready, TT * (q_.b - 1))
                for t in range(NB):
                    last = tr(V0[:, t * 128:(t + 1) * 128], vT[q_.s][:, t * BT:t * BT + 128], ident)
                last.then_inc(vwin_mm, 1)

            def far_weights(q_):
                for t in range(TT):
                    last = tr(V1[0:HEADS * NFAR, t * 128:(t + 1) * 128], attnf[q_.s][:, t, :], ident)
                last.then_inc(far_mm, 1)

            def spread_far(q_, which):
                if 0 in which:
                    pe.wait_ge(v2_ready, q_.b + 1)
                    pe.wait_ge(farT_ready, q_.b + 1)
                for i in which:
                    o = FAR[i]
                    if i >= 2:
                        pe.wait_ge(bc_used, NFAR * q_.b + i - 1)
                    mm((V0, V1)[i % 2][:, o:NP], P("pick", i * 128, (i + 1) * 128)[0:HEADS * NFAR, :],
                       farT[:, o:NP], start=True, stop=True).then_inc(bc_mm, 1)

            def attend(q_, between):
                pe.wait_ge(band_in, 16 * (q_.b + 1))
                groups = 2 * NB

                def turn_band(g):
                    t, half = divmod(g, 2)
                    if g < 2:
                        pe.wait_ge(bc_used, NFAR * q_.b + NFAR - 1 + g)
                    else:
                        pe.wait_ge(bandT_ready, groups * q_.b + g - 1)
                    for i in range(4):
                        col = (4 * half + (0, 2, 1, 3)[i]) * 128
                        last = tr((V0, V1)[g % 2][:, i * BT:(i + 1) * BT], band[:, t, col:col + 128],
                                  ident[0:BT, 0:BT])
                    last.then_inc(bandT_mm, 1)

                turn_band(0)
                after(pe, room_ready, q_.b)
                for g in range(groups):
                    t, half = divmod(g, 2)
                    if g + 1 < groups:
                        turn_band(g + 1)
                    between(g)
                    pe.wait_ge(bandT_ready, groups * q_.b + g + 1)
                    for i in range(4):
                        hh = 4 * half + (0, 2, 1, 3)[i]
                        rows = 32 * (hh // 2)
                        last = mm(V2[rows:rows + 32, t * BT:(t + 1) * BT], v2[:, t, hh, :],
                                  bandT[g % 2][:, i * BT:(i + 1) * BT], start=(hh % 2 == 0), stop=(hh % 2 == 1))
                    last.then_inc(pv_mm, 1)

            def out_project(q_):
                pe.wait_ge(ao_ready, q_.b + 1)
                mm(V0[:, 0:NP], P("outw"), ao[:, :], start=True, stop=True).then_inc(out_mm, 1)

            def center2(q_):
                pe.wait_ge(h2_ready, q_.b + 1)
                mm(V1[:, 0:NP], P("cen"), h2[q_.s][:, :], start=True, stop=True).then_inc(hc2_mm, 1)

            def variance2(q_):
                pe.wait_ge(sq2_ready, q_.b + 1)
                mm(V0[:, 0:NP], P("avg"), stat2[:, :], start=True, stop=True).then_inc(var2_mm, 1)

            def logits(q_):
                pe.wait_ge(x2_ready, q_.b + 1)
                after(pe, y1_ready, q_.b)
                for t in range(TT):
                    last = mm(V2[:, t * EXPERTS:(t + 1) * EXPERTS], x2[:, t * 128:(t + 1) * 128], P("router"),
                              start=True, stop=True)
                last.then_inc(logit_mm, 1)

            def up(q_, f, T, S_):
                if f == 0:
                    after(pe, gelu_ready, FC * q_.b)
                    if S_:
                        pe.wait_ge(gate_ready, S_.b + 1)
                elif f < FC - 1:
                    pe.wait_ge(gelu_ready, FC * q_.b + f)
                elif T:
                    pe.wait_ge(o_ready, T.b + 1)
                elif S_:
                    pe.wait_ge(k_ready, S_.b + 1)
                mm((T1 if f < FC - 1 else T0)[:, 0:NP], P("up", f * 128, (f + 1) * 128), x2[:, :],
                   start=True, stop=True).then_inc(up_mm, 1)

            def positions(q_):
                pe.wait_ge(msk_ready, q_.b + 1)
                pos = TT * EXPERTS
                for t in range(TT):
                    dst = V2[:, pos + t * EXPERTS:pos + (t + 1) * EXPERTS]
                    for u in range(t):
                        mm(dst, onesb[:, :], msk[:, u, :], start=(u == 0), stop=False)
                    mm(dst, beforeb[:, :], msk[:, t, :], start=(t == 0), stop=True)
                for t in range(TT):
                    rows = min(128, N - t * 128)
                    last = mm(V2[:, 2 * pos:2 * pos + EXPERTS], onesb[0:rows, :], msk[0:rows, t, :],
                              start=(t == 0), stop=(t == TT - 1))
                last.then_inc(pos_mm, 1)

            def down(q_, V, tiles):
                if 0 in tiles:
                    if V:
                        pe.wait_ge(o1_ready, V.b + 1)
                    else:
                        pe.wait_ge(room_ready, q_.b + 1)
                    pe.wait_ge(gelu_ready, FC * (q_.b + 1))
                for t in tiles:
                    for f in range(FC):
                        last = mm(V2[:, t * D:(t + 1) * D], hid[:, f, t * 128:(t + 1) * 128],
                                  P("down", f * D, (f + 1) * D), start=(f == 0), stop=(f == FC - 1))
                if TT - 1 in tiles:
                    last.then_inc(down_mm, 1)

            def turn_h2(q_, V):
                if V:
                    pe.wait_ge(lnv2_ready, V.b + 1)
                else:
                    pe.wait_ge(out_ready, TT * q_.b)
                for t in range(TT):
                    last = tr(V0[:, t * 128:(t + 1) * 128], h2[q_.s][:, t * 128:(t + 1) * 128], ident)
                last.then_inc(h2_turned, 1)

            def turn(T, S_, V, F):
                if T:
                    turn_x(T)
                if S_:
                    project_v(S_)
                if T:
                    convolve(T, 0)
                if F:
                    logits(F)
                if S_:
                    project_gate(S_)
                if F:
                    up(F, 0, T, S_)
                if S_:
                    score(S_, 0, range(1))
                if T:
                    convolve(T, 1)
                if F:
                    up(F, 1, T, S_)
                if V:
                    turn_values(V)
                    far_weights(V)
                if T:
                    convolve(T, 2)
                if F:
                    up(F, 2, T, S_)
                    positions(F)
                if S_:
                    score(S_, 0, range(1, 2))
                if F:
                    up(F, 3, T, S_)
                if S_:
                    score(S_, 2)
                if V:
                    spread_far(V, range(2))
                if S_:
                    score(S_, 0, range(2, 3))
                if V:
                    spread_far(V, range(2, 4))
                if S_:
                    score(S_, 0, range(3, 4))
                if V:
                    spread_far(V, range(4, 6))
                if T:
                    center(T, F)
                if S_:
                    score(S_, 1, range(1))
                if T:
                    variance(T, S_)

                def between(g):
                    if S_ and g in (1, 5):
                        score(S_, 1, range(g // 4 + 1, g // 4 + 2))
                    if T and g == 3:
                        project_qk(T)
                if V:
                    attend(V, between)
                else:
                    for g in range(2 * NB):
                        between(g)
                if S_:
                    score(S_, 1, range(3, 4))
                if V:
                    out_project(V)
                if F:
                    down(F, V, range(1))
                if V:
                    center2(V)
                if S_:
                    turn_scores(S_)
                if V:
                    variance2(V)
                if F:
                    down(F, V, range(1, TT))
                    turn_h2(F, V)
            pipeline(pe, turn)

        @block.scalar
        def _(act):
            A = nc.scalar.activation

            def bias(c):
                return P("bias", c, c + 1)
            act.wait_ge(par_in, 48)
            act.wait_ge(setup_dve, 1)
            act.wait_ge(pads_zero, 1)

            def copy_qk(q_):
                act.wait_ge(q_mm, q_.b + 1)
                after(act, fprod_used, q_.b - 1)
                A(q[q_.s][:, :], T1[:, 0:NP], ACT.Identity, bias=bias(BQ)).then_inc(q_ready, 1)
                act.wait_ge(k_mm, q_.b + 1)
                A(k[q_.s][:, KPAD:KPAD + NP], T0[:, 0:NP], ACT.Identity, bias=bias(BK)).then_inc(k_ready, 1)

            def copy_v(q_):
                act.wait_ge(v_mm, q_.b + 1)
                after(act, ao_ready, q_.b - 1)
                A(vT[q_.s][:, LOCAL:LOCAL + NP], T1[:, 0:NP], ACT.Identity, bias=bias(BV)).then_inc(v_ready, 1)

            def tanh_gate(q_):
                act.wait_ge(gate_mm, q_.b + 1)
                A(gate[q_.s][:, :], T1[:, 0:NP], ACT.Tanh, bias=hbias[:, BG:BG + 1], scale=0.5)\
                    .then_inc(gate_ready, 1)

            def copy_x(q_):
                act.wait_ge(x_turned, q_.b + 1)
                after(act, o_mm, q_.b)
                A(xT[:, 0:ROWS], T0[:, 0:ROWS], ACT.Copy).then_inc(xT_ready, 1)

            def tanh_z(q_):
                act.wait_ge(z_mm, q_.b + 1)
                after(act, h_ready, q_.b)
                A(zt[:, :], T0[:, 0:NP], ACT.Tanh, bias=bias(BZ)).then_inc(z_ready, 1)

            def tanh_f(q_):
                act.wait_ge(f_mm, q_.b + 1)
                A(ft[:, :], T0[:, 0:NP], ACT.Tanh, bias=hbias[:, BF:BF + 1], scale=0.5).then_inc(f_ready, 1)

            def tanh_o(q_):
                act.wait_ge(o_mm, q_.b + 1)
                A(ot[:, :], T0[:, 0:NP], ACT.Tanh, bias=hbias[:, BO:BO + 1], scale=0.5).then_inc(o_ready, 1)

            def norm_square(q_):
                act.wait_ge(hc_mm, q_.b + 1)
                after(act, xn_ready, q_.b)
                A(stat[:, :], T0[:, 0:NP], ACT.Square).then_inc(sq_ready, 1)

            def norm1_ln(q_):
                act.wait_ge(var_mm, q_.b + 1)
                A(stat[:, :], T1[:, 0:NP], ACT.Ln, bias=epsc[:, 0:1]).then_inc(lnv_ready, 1)

            def norm1_exp(q_):
                act.wait_ge(lnv_ready, q_.b + 1)
                A(stat[:, :], stat[:, :], ACT.Exp, scale=-0.5).then_inc(rstd_ready, 1)

            def norm2_square(q_):
                act.wait_ge(hc2_mm, q_.b + 1)
                after(act, x2_ready, q_.b)
                A(stat2[:, :], V1[:, 0:NP], ACT.Square).then_inc(sq2_ready, 1)

            def norm2(q_):
                act.wait_ge(var2_mm, q_.b + 1)
                A(stat2[:, :], V0[:, 0:NP], ACT.Ln, bias=epsc[:, 0:1]).then_inc(lnv2_ready, 1)
                act.wait_ge(lnv2_ready, q_.b + 1)
                A(stat2[:, :], stat2[:, :], ACT.Exp, scale=-0.5).then_inc(rstd2_ready, 1)

            def softmax_exp(q_):
                act.wait_ge(sub_ready, q_.b + 1)
                after(act, attn_ready, q_.b)
                A(ex[:, :, :], sc[:, :, :], ACT.Exp).then_inc(ex_ready, 1)

            def score_copy(q_, c):
                act.wait_ge(prod_used[c] if c < CH else fprod_used, q_.b + 1)
                after(act, scores_mm, TT * q_.b)
                rows = min(128, (NO - c * CW + 3) // 4 * 32)
                A(scT[0:rows, c, 0:N], S[c][0:rows, 0:N], ACT.Copy).then_inc(scT_ready, 1)

            def value_blocks(q_):
                act.wait_ge(vwin_mm, q_.b + 1)
                after(act, pv_mm, 2 * NB * q_.b)
                for t in range(NB):
                    dst = bass.AP(v2[:, :, :, :].tensor, t * HEADS * 32,
                                  [[NB * HEADS * 32, 128], [64, HEADS // 2], [32 + HD, 2], [1, HD]])
                    last = A(dst, V0[:, t * 128:(t + 1) * 128].rearrange("p (i e d) -> p i e d", e=2, d=HD), ACT.Copy)
                last.then_inc(v2_ready, 1)

            def far_copy(q_):
                act.wait_ge(far_mm, q_.b + 1)
                after(act, bc_mm, NFAR * q_.b)
                A(farT[:, :], V1[0:HEADS * NFAR, 0:NP], ACT.Copy).then_inc(farT_ready, 1)

            def band_copies(q_, groups):
                for g in groups:
                    act.wait_ge(bandT_mm, 2 * NB * q_.b + g + 1)
                    after(act, pv_mm, 2 * NB * q_.b + g - 1)
                    A(bandT[g % 2][:, :], (V0, V1)[g % 2][:, 0:4 * BT], ACT.Copy).then_inc(bandT_ready, 1)

            def router_exp(q_):
                act.wait_ge(lsub_ready, q_.b + 1)
                after(act, kw_ready, q_.b)
                A(exr[:, :, :], lsub[:, :, :], ACT.Exp).then_inc(exr_ready, 1)

            def gelu(q_, f):
                if f == 0:
                    after(act, down_mm, q_.b)
                act.wait_ge(up_mm, FC * q_.b + f + 1)
                A(hid[:, f, :], (T1 if f < FC - 1 else T0)[:, 0:NP], ACT.Gelu, bias=bias(B1 + f))\
                    .then_inc(gelu_ready, 1)

            def turn(T, S_, V, F):
                if T:
                    copy_x(T)
                if V:
                    softmax_exp(V)
                if S_:
                    copy_v(S_)
                act.preload_act_table_set("gelu_and_others")
                if T:
                    tanh_z(T)
                if S_:
                    tanh_gate(S_)
                if F:
                    gelu(F, 0)
                if T:
                    tanh_f(T)
                if F:
                    gelu(F, 1)
                if V:
                    far_copy(V)
                    value_blocks(V)
                if T:
                    tanh_o(T)
                if F:
                    gelu(F, 2)
                    gelu(F, 3)
                act.preload_act_table_set("natural_log_exp_and_others")
                if F:
                    router_exp(F)
                if S_:
                    score_copy(S_, 2)
                    score_copy(S_, 0)
                if T:
                    norm_square(T)
                    norm1_ln(T)
                if V:
                    band_copies(V, range(2))
                if T:
                    norm1_exp(T)
                if V:
                    band_copies(V, range(2, 5))
                if T:
                    copy_qk(T)
                if V:
                    band_copies(V, range(5, 2 * NB))
                if S_:
                    score_copy(S_, 1)
                if V:
                    norm2_square(V)
                    norm2(V)
            pipeline(act, turn)

        @block.vector
        def _(dve):
            v = nc.vector
            dve.wait_ge(par_in, 48)
            v.tensor_scalar(hbias[:, :], P("bias"), 0.5, None, ALU.mult)
            v.memset(epsc[:, :], EPS)
            v.memset(room[:, :], float(CAP))
            v.tensor_copy(beforeb[:, :], P("before"))
            v.tensor_copy(onesb[:, :], P("ones"))
            v.tensor_scalar(gain2[:, :], P("gain"), 0.5, None, ALU.mult)
            v.tensor_scalar(se1[:, :], P("se"), 1.0, HD ** -0.5, ALU.add, ALU.mult).then_inc(setup_lin, 1)
            dve.wait_ge(setup_lin, 1)
            for r in range(4):
                n = (NO - r + 3) // 4
                v.tensor_tensor(bass.AP(ew[:, :, :].tensor, r * 32, [[NO * 32, 128], [4 * 32, n], [1, 32]]),
                                bass.AP(se1[:, :].tensor, r, [[NO, 128], [4, n], [0, 32]]),
                                P("ind", r * 32, (r + 1) * 32).unsqueeze(1).broadcast_to([128, n, 32]), ALU.mult)
            oh = P("cosk").rearrange("p (h o) -> p h o", o=NO)
            v.tensor_tensor(bias_oh, oh, P("amp").unsqueeze(2).broadcast_to([128, HEADS, NO]), ALU.mult)\
                .then_inc(setup_lin, 1)
            dve.wait_ge(setup_lin, 2)
            v.tensor_tensor(bias_oh, bias_oh, P("pos").rearrange("p (h o) -> p h o", o=NO), ALU.add)\
                .then_inc(setup_lin, 1)
            dve.wait_ge(setup_lin, 3)
            for t in range(TT):
                last = v.tensor_tensor(bm[:, t, :, :], bias_oh,
                                       P("mask", t * NO, (t + 1) * NO).unsqueeze(1).broadcast_to([128, HEADS, NO]),
                                       ALU.add)
            last.then_inc(setup_dve, 1)
            dve.wait_ge(setup_dve, 1)
            dve.wait_ge(pads_zero, 1)

            def recur(q_):
                dve.wait_ge(z_ready, q_.b + 1)
                dve.wait_ge(f_ready, q_.b + 1)
                v.tensor_scalar(forget[:, :], ft[:, :], 0.5, 0.5, ALU.mult, ALU.add)
                v.scalar_tensor_tensor(mixin[:, :], ft[:, :], 1.0, zt[:, :], ALU.subtract, ALU.mult)\
                    .then_inc(mixin_ready, 1)
                dve.wait_ge(mixin_ready, q_.b + 1)
                v.tensor_tensor_scan(cell[:, :], forget[:, :], mixin[:, :], 0.0, ALU.mult, ALU.add)\
                    .then_inc(c_ready, 1)
                dve.wait_ge(c_ready, q_.b + 1)
                dve.wait_ge(o_ready, q_.b + 1)
                after(dve, hkeep_ready, q_.b - 1)
                v.scalar_tensor_tensor(h[q_.s][:, :], ot[:, :], 1.0, cell[:, :], ALU.add, ALU.mult)\
                    .then_inc(h_ready, 1)

            def norm1(q_):
                dve.wait_ge(rstd_ready, q_.b + 1)
                after(dve, gate_ready, q_.b - 1)
                v.tensor_tensor(xn[q_.s][:, :], T0[:, 0:NP], stat[:, :], ALU.mult).then_inc(xn_ready, 1)

            def products(q_, c, part):
                if part == 0:
                    dve.wait_ge(k_ready, q_.b + 1)
                    after(dve, prod_used[c], q_.b)
                w = CW // PARTS
                back = bass.AP(k[q_.s][:, :].tensor, KPAD - LOCAL + c * CW + part,
                               [[KPAD + NP, 128], [PARTS, w], [1, N]])
                v.tensor_tensor(bass.AP(prod[c][:, :, :].tensor, part * N, [[CW * N, 128], [PARTS * N, w], [1, N]]),
                                q[q_.s][:, 0:N].unsqueeze(1).broadcast_to([128, w, N]), back,
                                ALU.mult).then_inc(prod_ready[c], 1)

            def softmax_in(q_):
                for t in range(TT):
                    dve.wait_ge(scores_mm, TT * q_.b + t + 1)
                    v.tensor_tensor(sc[:, t * HEADS:(t + 1) * HEADS, :],
                                    S[t][:, 0:SC].rearrange("p (o h) -> p h o", h=HEADS), bm[:, t, :, :],
                                    ALU.add).then_inc(sc_ready, 1)
                dve.wait_ge(sc_ready, TT * (q_.b + 1))
                v.tensor_reduce(mx[:, :], sc[:, :, :], AX.X, ALU.max).then_inc(mx_ready, 1)
                dve.wait_ge(mx_ready, q_.b + 1)
                v.tensor_tensor(sc[:, :, :], sc[:, :, :], mx[:, :].unsqueeze(2).broadcast_to([128, TT * HEADS, NO]),
                                ALU.subtract).then_inc(sub_ready, 1)

            def softmax_out(q_):
                dve.wait_ge(ex_ready, q_.b + 1)
                v.tensor_reduce(sm[:, :], ex[:, :, :], AX.X, ALU.add).then_inc(sm_ready, 1)
                dve.wait_ge(sm_ready, q_.b + 1)
                v.reciprocal(rs[:, :], sm[:, :]).then_inc(rc_ready, 1)
                dve.wait_ge(rc_ready, q_.b + 1)
                rs3 = rs[:, :].rearrange("p (t h) -> p t h", h=HEADS)
                v.tensor_tensor(rs3, rs3, gain2[:, :].unsqueeze(1).broadcast_to([128, TT, HEADS]), ALU.mult)\
                    .then_inc(rs_ready, 1)
                dve.wait_ge(rs_ready, q_.b + 1)
                after(dve, band_out[q_.s], 96 * q_.g)
                after(dve, farT_ready, q_.b - 1)
                v.tensor_tensor(attn[q_.s][:, :, :, :].rearrange("p t h o -> p (t h) o"), ex[:, :, 0:DENSE],
                                rs[:, :].unsqueeze(2).broadcast_to([128, TT * HEADS, DENSE]), ALU.mult)
                v.tensor_tensor(attnf[q_.s][:, :, :].rearrange("p t (h o) -> p (t h) o", o=NFAR), ex[:, :, DENSE:NO],
                                rs[:, :].unsqueeze(2).broadcast_to([128, TT * HEADS, NFAR]), ALU.mult)\
                    .then_inc(attn_ready, 1)

            def far_values(q_):
                for i, o in enumerate(FAR):
                    dve.wait_ge(bc_mm, NFAR * q_.b + i + 1)
                    if 1 <= i:
                        after(dve, acc_added, (NFAR - 1) * q_.b + (i - 2 if i > 2 else 0))
                    dst = acc if i == 0 else tmp[i % 2]
                    v.tensor_tensor(dst[:, o:NP], (V0, V1)[i % 2][:, o:NP], vT[q_.s][:, LOCAL:LOCAL + NP - o],
                                    ALU.mult).then_inc(bc_used, 1)

            def attention_out(q_):
                dve.wait_ge(pv_mm, 2 * NB * (q_.b + 1))
                dve.wait_ge(acc_added, (NFAR - 1) * (q_.b + 1))
                v.tensor_tensor(o1[:, :], V2[:, 0:NP], acc[:, :], ALU.add).then_inc(o1_ready, 1)
                dve.wait_ge(o1_ready, q_.b + 1)
                v.scalar_tensor_tensor(ao[:, :], gate[q_.s][:, :], 1.0, o1[:, :], ALU.add, ALU.mult)\
                    .then_inc(ao_ready, 1)

            def residual(q_):
                dve.wait_ge(out_mm, q_.b + 1)
                dve.wait_ge(hkeep_ready, q_.b + 1)
                after(dve, h2_turned, q_.b - 1)
                v.scalar_tensor_tensor(h2[q_.s][:, :], V0[:, 0:NP], P("bias", BOUT, BOUT + 1), hkeep[q_.s][:, :],
                                       ALU.add, ALU.add).then_inc(h2_ready, 1)

            def norm2(q_):
                dve.wait_ge(rstd2_ready, q_.b + 1)
                after(dve, up_mm, FC * q_.b)
                v.tensor_tensor(x2[:, :], V1[:, 0:NP], stat2[:, :], ALU.mult).then_inc(x2_ready, 1)

            def route(q_):
                dve.wait_ge(logit_mm, q_.b + 1)
                v.tensor_copy(lg[:, :, :], V2[:, 0:TT * EXPERTS].rearrange("p (t e) -> p t e", e=EXPERTS))\
                    .then_inc(lg_ready, 1)
                dve.wait_ge(lg_ready, q_.b + 1)
                v.tensor_reduce(lmax[:, :], lg[:, :, :], AX.X, ALU.max).then_inc(lmax_ready, 1)
                for t in range(TT):
                    last = v.max(m8[:, t, :], lg[:, t, :])
                last.then_inc(m8_ready, 1)
                dve.wait_ge(lmax_ready, q_.b + 1)
                dve.wait_ge(m8_ready, q_.b + 1)
                v.tensor_tensor(lsub[:, :, :], lg[:, :, :], lmax[:, :].unsqueeze(2).broadcast_to([128, TT, EXPERTS]),
                                ALU.subtract).then_inc(lsub_ready, 1)

            def route_picks(q_):
                for t in range(TT):
                    last = v.max_index(i8[:, t, :], m8[:, t, :], lg[:, t, :])
                last.then_inc(i8_ready, 1)
                dve.wait_ge(i8_ready, q_.b + 1)
                v.tensor_copy(idf[:, :, :], i8[:, :, 0:TOPK]).then_inc(idf_ready, 1)
                dve.wait_ge(idf_ready, q_.b + 1)
                iota = P("iota").unsqueeze(1).broadcast_to([128, TT, EXPERTS])
                v.tensor_tensor(eq0[:, :, :], iota, idf[:, :, 0:1].broadcast_to([128, TT, EXPERTS]), ALU.is_equal)
                v.tensor_tensor(eq1[:, :, :], iota, idf[:, :, 1:2].broadcast_to([128, TT, EXPERTS]), ALU.is_equal)\
                    .then_inc(eq_ready, 1)
                dve.wait_ge(eq_ready, q_.b + 1)
                v.tensor_tensor(msk[:, :, :], eq0[:, :, :], eq1[:, :, :], ALU.add).then_inc(msk_ready, 1)

            def keep(q_):
                dve.wait_ge(pos_mm, q_.b + 1)
                v.tensor_tensor(kept[:, :, :], V2[:, TT * EXPERTS:2 * TT * EXPERTS].rearrange("p (t e) -> p t e", e=EXPERTS),
                                room[:, :].unsqueeze(1).broadcast_to([128, TT, EXPERTS]), ALU.is_lt)\
                    .then_inc(kept_ready, 1)
                dve.wait_ge(kept_ready, q_.b + 1)
                v.tensor_tensor(room[:, :], room[:, :], V2[:, 2 * TT * EXPERTS:(2 * TT + 1) * EXPERTS], ALU.subtract)\
                    .then_inc(room_ready, 1)
                v.tensor_tensor(kept[:, :, :], kept[:, :, :], msk[:, :, :], ALU.mult).then_inc(kept2_ready, 1)

            def weigh(q_):
                dve.wait_ge(kept2_ready, q_.b + 1)
                dve.wait_ge(exr_ready, q_.b + 1)
                v.tensor_tensor(kw[:, :, :], kept[:, :, :], exr[:, :, :], ALU.mult)
                v.tensor_reduce(smr[:, :], exr[:, :, :], AX.X, ALU.add).then_inc(kw_ready, 1)
                dve.wait_ge(kw_ready, q_.b + 1)
                v.tensor_reduce(gs[:, :], kw[:, :, :], AX.X, ALU.add)
                v.reciprocal(rcr[:, :], smr[:, :]).then_inc(gs_ready, 1)
                dve.wait_ge(gs_ready, q_.b + 1)
                v.tensor_tensor(gt[:, :], gs[:, :], rcr[:, :], ALU.mult).then_inc(gt_ready, 1)

            def finish(q_):
                dve.wait_ge(down_mm, q_.b + 1)
                v.tensor_tensor(y1[:, :, :], V2[:, 0:TT * D].rearrange("p (t d) -> p t d", d=D),
                                P("b2").unsqueeze(1).broadcast_to([128, TT, D]), ALU.add).then_inc(y1_ready, 1)
                dve.wait_ge(y1_ready, q_.b + 1)
                dve.wait_ge(gt_ready, q_.b + 1)
                dve.wait_ge(h2_turned, q_.b + 1)
                after(dve, out_stored[q_.s], 32 * q_.g)
                for t in range(TT):
                    v.scalar_tensor_tensor(osb[q_.s][:, t, :], y1[:, t, :], gt[:, t:t + 1],
                                           V0[:, t * D:(t + 1) * D], ALU.mult, ALU.add).then_inc(out_ready, 1)

            def turn(T, S_, V, F):
                if V:
                    softmax_out(V)
                if S_:
                    products(S_, 0, 3)
                if F:
                    route(F)
                    route_picks(F)
                if S_:
                    products(S_, 1, 0)
                if F:
                    keep(F)
                if S_:
                    products(S_, 1, 1)
                if T:
                    recur(T)
                if V:
                    far_values(V)
                if S_:
                    products(S_, 1, 2)
                if T:
                    norm1(T)
                if S_:
                    products(S_, 1, 3)
                if T:
                    products(T, 0, 0)
                    products(T, 0, 1)
                if V:
                    attention_out(V)
                if F:
                    weigh(F)
                if V:
                    residual(V)
                if T:
                    products(T, 0, 2)
                if S_:
                    softmax_in(S_)
                if V:
                    norm2(V)
                if F:
                    finish(F)
            pipeline(dve, turn)

        @block.gpsimd
        def _(pool):
            g = nc.gpsimd
            g.memset(xT[:, ROWS:NP + 1], 0.0)
            g.memset(back4[:, :], -0.25)
            for s in range(2):
                g.memset(k[s][:, 0:KPAD], 0.0)
                g.memset(vT[s][:, 0:LOCAL], 0.0)
            g.memset(scT[:, :, N:NP], 0.0)
            g.memset(fprod[:, :, :], 0.0)
            g.memset(acc[:, 0:FAR[0]], 0.0)
            g.memset(v2[:, :, :, :], 0.0).then_inc(pads_zero, 1)
            pool.wait_ge(pads_zero, 1)

            def carry(q_):
                pool.wait_ge(h_ready, q_.b + 1)
                after(pool, h2_ready, q_.b - 1)
                g.tensor_tensor(hkeep[q_.s][:, :], h[q_.s][:, :], back4[:, :].broadcast_to([128, NP]), ALU.mult)\
                    .then_inc(hkeep_ready, 1)

            def far_products(q_):
                pool.wait_ge(k_ready, q_.b + 1)
                after(pool, fprod_used, q_.b)
                for i, o in enumerate(OFFS[CH * CW:]):
                    last = g.tensor_tensor(fprod[:, i, o:N], q[q_.s][:, o:N], k[q_.s][:, KPAD:KPAD + N - o], ALU.mult)
                last.then_inc(fprod_ready, 1)

            def far_sum(q_):
                for i in range(1, NFAR):
                    o = FAR[i]
                    pool.wait_ge(bc_used, NFAR * q_.b + i + 1)
                    after(pool, acc_added, (NFAR - 1) * q_.b + i - 1)
                    g.tensor_tensor(acc[:, o:NP], acc[:, o:NP], tmp[i % 2][:, o:NP], ALU.add).then_inc(acc_added, 1)

            def turn(T, S_, V, F):
                if S_:
                    carry(S_)
                if S_:
                    far_products(S_)
                if V:
                    far_sum(V)
            pipeline(pool, turn)


def _params(i):
    f = np.float32
    a = {}
    a["ident"] = np.eye(128, dtype=f)
    a["conv"] = np.concatenate([i["L0_tok_W_" + g][:, :, t].T for g in "zfo" for t in range(2)], axis=1)
    cols = [i["L0_tok_b_" + g][:, None] for g in "zfo"]
    qb = i["L0_attn_b_qkv"]
    cols += [qb[D * t:D * (t + 1), None] for t in range(3)]
    cols += [i["L0_attn_b_gate"][:, None], i["L0_attn_b_out"][:, None], i["L0_ffn_b1"].reshape(FC, 128).T]
    a["bias"] = np.concatenate(cols, axis=1)
    a["cen"] = (np.eye(128) - 1.0 / 128).astype(f)
    a["cen4"] = a["cen"] * f(-0.25)
    a["avg"] = np.full((128, 128), 1.0 / 128, f)
    a["qkv"] = i["L0_attn_W_qkv"]
    a["gatew"] = i["L0_attn_W_gate"]
    order = OFFS_INDEX
    a["se"] = np.tile(i["L0_attn_scale_embed"][order].T, (HEADS, 1))
    ch = np.arange(128)
    col = np.arange(32)[None, None, :]
    a["ind"] = (col == 8 * np.arange(4)[None, :, None] + ch[:, None, None] // HD).astype(f).reshape(128, 128)
    a["pos"] = np.broadcast_to(i["L0_attn_pos_bias"][order].T.reshape(1, SC), (128, SC))
    log_max = np.log(1.0 + 4096.0)
    om = np.array([0.0, 0.0, 1, 1, 4, 4, 6, 6]) * np.pi / log_max
    logd = np.log(1.0 + np.array(OFFS, np.float64))
    cosk = np.where(om[:, None] > 0, np.cos(om[:, None] * logd[None, :]), 0.0).astype(f)
    a["cosk"] = np.broadcast_to(cosk.reshape(1, SC), (128, SC))
    a["amp"] = np.broadcast_to(i["L0_attn_disp_amp"][None, :], (128, HEADS))
    a["gain"] = np.broadcast_to(i["L0_attn_if_gain"][None, :], (128, HEADS))
    tok = ch[:, None, None] + 128 * np.arange(TT)[None, :, None]
    a["mask"] = np.where(tok >= np.array(OFFS)[None, None, :], 0.0, MASKED).astype(f).reshape(128, TT * NO)
    pick = np.zeros((128, NFAR, 128), f)
    for hh in range(HEADS):
        for s in range(NFAR):
            pick[hh * NFAR + s, s, hh * HD:(hh + 1) * HD] = 1.0
    a["pick"] = pick.reshape(128, NFAR * 128)
    a["outw"] = i["L0_attn_W_out"]
    a["router"] = i["L0_ffn_router_w"].T
    a["up"] = i["L0_ffn_w1"].T
    a["down"] = i["L0_ffn_w2"].T.reshape(FC, 128, D).transpose(1, 0, 2).reshape(128, FC * D)
    a["b2"] = np.broadcast_to(i["L0_ffn_b2"][None, :], (128, D))
    a["iota"] = np.broadcast_to(np.arange(EXPERTS, dtype=f)[None, :], (128, EXPERTS))
    a["before"] = (ch[:, None] < ch[None, :]).astype(f)
    a["ones"] = np.ones((128, 128), f)
    for n, w in FIELDS + SETUP:
        assert a[n].shape == (128, w), (n, a[n].shape)
    return np.ascontiguousarray(np.concatenate([a[n] for n, _ in FIELDS + SETUP], axis=1))


OFFS_INDEX = [LOCAL - j for j in range(DENSE)] + [DENSE + s for s in range(NFAR)]


def kernel(**inputs):
    import concourse.bacc as _bacc
    from concourse.bass_utils import run_bass_kernel_spmd as _run

    i = {n: np.asarray(a) for n, a in inputs.items()}
    arrays = {"x_dram": np.ascontiguousarray(i["x"]), "params_dram": _params(i)}
    nc = _bacc.Bacc("TRN2", target_bir_lowering=False, num_devices=1)
    f32 = mybir.dt.float32
    x = nc.dram_tensor("x_dram", [BATCH, ROWS, D], f32, kind="ExternalInput").ap()
    params = nc.dram_tensor("params_dram", [128, ALLCOLS], f32, kind="ExternalInput").ap()
    out = nc.dram_tensor("out_dram", [BATCH, N, D], f32, kind="ExternalOutput").ap()
    build(nc, x, params, out)
    r = _run(nc, [arrays], core_ids=[0])
    return r.results[0]["out_dram"]
```

```python
import numpy as np
import concourse.bass as bass
from concourse import mybir
from contextlib import ExitStack

BATCH, ROWS, D = 16, 375, 128
N = ROWS - 1
NP = 384
TT = NP // 128
BT, NB = 96, NP // 96
HEADS, HD = 8, 16
LOCAL = 32
DENSE = LOCAL + 1
FAR = [48, 64, 96, 128, 192, 256]
NFAR = len(FAR)
OFFS = [LOCAL - j for j in range(DENSE)] + FAR
NO = len(OFFS)
CW = 16
CG = 4
CH = NO // CW
POOL_PARTS = (2, 3)
PARTS = 4
LAST = NO - CH * CW
LSTEPS = -(-LAST // CG)
KPAD = max(FAR)
SC = HEADS * NO
FH = HEADS * NFAR // 2
EXPERTS, TOPK, CAP, FFN = 64, 2, 128, 512
FC = FFN // 128
EPS = 1e-5
MASKED = -1e30
XT = 125

FIELDS = [
    ("ident", 128), ("conv", 6 * D), ("bias", 12),
    ("cen", 128), ("cen4", 128), ("avg", 128),
    ("qkv", 3 * D), ("gatew", D),
    ("se", NO), ("ind", 4 * 32), ("amp", HEADS), ("gain", HEADS), ("pick", NFAR * 128), ("outw", D), ("router", EXPERTS), ("up", FFN), ("down", FC * D), ("b2", D),
    ("iota", EXPERTS), ("before", 128), ("ones", 128),
]
SETUP = [("pos", SC), ("cosk", SC), ("mask", TT * NO)]
COL, _at = {}, 0
for _n, _w in FIELDS:
    COL[_n] = (_at, _at + _w)
    _at += _w
PCOLS = _at
for _n, _w in SETUP:
    COL[_n] = (_at, _at + _w)
    _at += _w
ALLCOLS = _at
BZ, BF, BO, BQ, BK, BV, BG, BOUT, B1 = 0, 1, 2, 3, 4, 5, 6, 7, 8


class Seq:

    def __init__(self, b, s, g):
        self.b, self.s, self.g = b, s, g


def build(nc, x, params, out):
    fp32, bf16, u32 = mybir.dt.float32, mybir.dt.bfloat16, mybir.dt.uint32
    ALU, ACT, AX = mybir.AluOpType, mybir.ActivationFunctionType, mybir.AxisListType
    band_dram = nc.dram_tensor("band_scratch", [2, NP, HEADS * 128], fp32, kind="Internal").ap()

    with ExitStack() as ctx:
        def sb(name, shape, dt=fp32):
            return ctx.enter_context(nc.sbuf_tensor(name, shape, dt))

        def bank(name):
            return ctx.enter_context(nc.psum_tensor(name, [128, 512], fp32))

        def sem(name):
            return ctx.enter_context(nc.semaphore(name))

        par = sb("par", [128, PCOLS])

        def P(name, a=0, b=None):
            lo, hi = COL[name]
            if lo >= PCOLS:
                flat = attn[0][:, :, :, :].rearrange("p t h o -> p (t h o)")
                return flat[:, lo - PCOLS + a:(hi if b is None else lo + b) - PCOLS]
            return par[:, lo + a:(hi if b is None else lo + b)]

        xin = [sb(f"xin{s}", [XT, 3, D]) for s in range(2)]
        xT = sb("xT", [128, ROWS])
        zt, ft, ot = sb("zt", [128, N]), sb("ft", [128, N]), sb("ot", [128, N])
        forget, mixin, cell = sb("forget", [128, N]), sb("mixin", [128, N]), sb("cell", [128, N])
        back4 = sb("back4", [128, 1])
        h = [sb(f"h{s}", [128, N]) for s in range(2)]
        hkeep = [sb(f"hkeep{s}", [128, N]) for s in range(2)]
        stat = sb("stat", [128, N])
        xn = [sb(f"xn{s}", [128, N]) for s in range(2)]
        q = [sb(f"q{s}", [128, N]) for s in range(2)]
        k = [sb(f"k{s}", [128, KPAD + NP]) for s in range(2)]
        vT = [sb(f"vT{s}", [128, LOCAL + NP]) for s in range(2)]
        gate = [sb(f"gate{s}", [128, N]) for s in range(2)]
        prod = [sb(f"prod{c}", [128, CW, N]) for c in range(CH)]
        fprod = sb("fprod", [128, LAST, N])
        ew = sb("ew", [128, NO, 32])
        scT = sb("scT", [128, CH + 1, NP])
        bm = sb("bm", [128, TT, HEADS, NO])
        sc = sb("sc", [128, TT * HEADS, NO])
        ex = sb("ex", [128, TT * HEADS, NO])
        mx, sm, rs = sb("mx", [128, TT * HEADS]), sb("sm", [128, TT * HEADS]), sb("rs", [128, TT * HEADS])
        attn = [sb(f"attn{s}", [128, TT, HEADS, DENSE]) for s in range(2)]
        attnf = sb("attnf", [128, TT * 2, FH])
        rest = sb("rest", [128, TT * 2, FH])
        far3 = sb("far3", [128, TT * 2, 3, FH], bf16)
        band = sb("band", [BT, NB, HEADS * 128])
        bandT = [sb(f"bandT{i}", [128, 4 * BT]) for i in range(4)]
        v2 = sb("v2", [128, NB, HEADS, 32])
        farT = sb("farT", [3 * FH, 2, NP], bf16)
        identb, pickb = sb("identb", [128, 128], bf16), sb("pickb", [128, NFAR * 128], bf16)
        one = sb("one", [128, 1])
        acc = sb("acc", [128, N])
        tmp = [sb(f"tmp{i}", [128, N]) for i in range(2)]
        o1, ao = sb("o1", [128, N]), sb("ao", [128, N])
        h2 = [sb(f"h2{s}", [128, NP]) for s in range(2)]
        stat2, x2 = sb("stat2", [128, N]), sb("x2", [128, NP])
        lg, lsub, exr = (sb(n, [128, TT, EXPERTS]) for n in ("lg", "lsub", "exr"))
        m8 = sb("m8", [128, TT, 8])
        i8 = sb("i8", [128, TT, 8], u32)
        idf = sb("idf", [128, TT, TOPK])
        eq0, eq1 = sb("eq0", [128, TT, EXPERTS]), sb("eq1", [128, TT, EXPERTS])
        msk = sb("msk", [128, TT, EXPERTS], bf16)
        room = sb("room", [128, EXPERTS])
        kept, kw = sb("kept", [128, TT, EXPERTS]), sb("kw", [128, TT, EXPERTS])
        lmax, gs, smr, rcr, gt = (sb(n, [128, TT]) for n in ("lmax", "gs", "smr", "rcr", "gt"))
        beforeb, onesb = sb("beforeb", [128, 128], bf16), sb("onesb", [128, 128], bf16)
        hid = sb("hid", [128, FC, NP])
        y1 = sb("y1", [128, TT, D])
        osb = [sb(f"osb{s}", [128, TT, D]) for s in range(2)]
        hbias = sb("hbias", [128, 12])
        epsc = sb("epsc", [128, 1])
        se1 = sb("se1", [128, NO])
        gain2 = sb("gain2", [128, HEADS])
        bias_oh = attn[1][:, :, :, :].rearrange("p t h o -> p (t h o)")[:, 0:SC].rearrange("p (h o) -> p h o", o=NO)

        T0, T1 = bank("T0"), bank("T1")
        S = [bank(f"S{t}") for t in range(TT)]
        V0, V1, V2 = bank("V0"), bank("V1"), bank("V2")
        V1b = V1[:, :].bitcast(bf16)

        conv_in, par_in, scratch_zero = sem("conv_in"), sem("par_in"), sem("scratch_zero")
        pads_zero, zeros_ready, hbias_ready = sem("pads_zero"), sem("zeros_ready"), sem("hbias_ready")
        setup_dve, setup_lin, x_turned = sem("setup_dve"), sem("setup_lin"), sem("x_turned")
        xT_ready, z_mm, z_ready = sem("xT_ready"), sem("z_mm"), sem("z_ready")
        f_mm, f_ready, o_mm = sem("f_mm"), sem("f_ready"), sem("o_mm")
        o_ready, mixin_ready, c_ready = sem("o_ready"), sem("mixin_ready"), sem("c_ready")
        h_ready, hc_mm, sq_ready = sem("h_ready"), sem("hc_mm"), sem("sq_ready")
        var_mm, lnv_ready, rstd_ready = sem("var_mm"), sem("lnv_ready"), sem("rstd_ready")
        xn_ready, q_mm, q_ready = sem("xn_ready"), sem("q_mm"), sem("q_ready")
        k_mm, k_ready, v_mm = sem("k_mm"), sem("k_ready"), sem("v_mm")
        v_ready, gate_mm, gate_ready = sem("v_ready"), sem("gate_mm"), sem("gate_ready")
        hkeep_ready, scores_mm, sc_ready = sem("hkeep_ready"), sem("scores_mm"), sem("sc_ready")
        mx_ready, sub_ready, ex_ready = sem("mx_ready"), sem("sub_ready"), sem("ex_ready")
        sm_ready, rc_ready, rs_ready = sem("sm_ready"), sem("rc_ready"), sem("rs_ready")
        attn_ready, vwin_mm, v2_ready = sem("attn_ready"), sem("vwin_mm"), sem("v2_ready")
        far_mm, farT_ready, bc_mm = sem("far_mm"), sem("farT_ready"), sem("bc_mm")
        bc_used, acc_added, bandT_mm = sem("bc_used"), sem("acc_added"), sem("bandT_mm")
        bandT_ready, pv_mm, o1_ready = sem("bandT_ready"), sem("pv_mm"), sem("o1_ready")
        ao_ready, out_mm, h2_ready = sem("ao_ready"), sem("out_mm"), sem("h2_ready")
        hc2_mm, sq2_ready, var2_mm = sem("hc2_mm"), sem("sq2_ready"), sem("var2_mm")
        lnv2_ready, rstd2_ready, x2_ready = sem("lnv2_ready"), sem("rstd2_ready"), sem("x2_ready")
        logit_mm, lg_ready, lmax_ready = sem("logit_mm"), sem("lg_ready"), sem("lmax_ready")
        m8_ready, i8_ready, idf_ready = sem("m8_ready"), sem("i8_ready"), sem("idf_ready")
        eq_ready, msk_ready, pos_mm = sem("eq_ready"), sem("msk_ready"), sem("pos_mm")
        lsub_ready, exr_ready, smr_ready = sem("lsub_ready"), sem("exr_ready"), sem("smr_ready")
        kept_ready, room_ready = sem("kept_ready"), sem("room_ready")
        kept2_ready, kw_ready, gs_ready = sem("kept2_ready"), sem("kw_ready"), sem("gs_ready")
        gt_ready, up_mm, gelu_ready = sem("gt_ready"), sem("up_mm"), sem("gelu_ready")
        down_mm, y1_ready, h2_turned = sem("down_mm"), sem("y1_ready"), sem("h2_turned")
        out_ready = sem("out_ready")
        band_in = [sem(f"band_in{half}") for half in range(2)]
        attnf_ready = sem("attnf_ready")
        hi_ready, rest_ready, mid_ready, far3_ready = sem("hi_ready"), sem("rest_ready"), sem("mid_ready"), sem("far3_ready")
        scT_ready, pool_prod_ready = sem("scT_ready"), sem("pool_prod_ready")
        prod_ready = [sem(f"prod{c}_ready") for c in range(CH)]
        prod_used = [sem(f"prod{c}_used") for c in range(CH)]
        fprod_ready, fprod_used = sem("fprod_ready"), sem("fprod_used")
        x_in = [sem(f"x_in{s}") for s in range(2)]
        band_out = [[sem(f"band_out{half}{s}") for s in range(2)] for half in range(2)]
        out_stored = [sem(f"out_stored{s}") for s in range(2)]

        def after(eng, s, n):
            if isinstance(n, int) and n <= 0:
                return
            eng.wait_ge(s, n)

        def up_bank(f, T):
            return T0 if f == FC - 1 or (T is None and f % 2) else T1

        def is_first(q_):
            return isinstance(q_.b, int) and q_.b == 0

        def pipeline(eng, turn, lags=(0, 1, 2, 3)):
            def at(n):
                return Seq(n, n % 2, n // 2) if 0 <= n < BATCH else None
            for n in range(4):
                turn(*(at(n - lag) for lag in lags))
            with eng.Fori(0, (BATCH - 4) // 2) as i:
                for u in range(4, 6):
                    turn(*(Seq(i * 2 + u - lag, (u - lag) % 2, i + (u - lag) // 2) for lag in lags))
            for n in range(BATCH, BATCH + max(lags)):
                turn(*(at(n - lag) for lag in lags))

        block = ctx.enter_context(nc.Block())

        @block.sync
        def _(sp):
            cut = COL["cen"][0]
            sp.dma_start(par[:, 0:cut], params[:, 0:cut]).then_inc(conv_in, 16)
            def load_x(q_):
                after(sp, x_turned, q_.b - 1)
                sp.dma_start(xin[q_.s][:, :, :], x[q_.b, :, :].rearrange("(t p) d -> p t d", p=XT))\
                    .then_inc(x_in[q_.s], 16)

            def store_out(q_):
                sp.wait_ge(out_ready, TT * (q_.b + 1))
                full = 128 * (TT - 1)
                sp.dma_start(out[q_.b, 0:full, :].rearrange("(t p) d -> p t d", p=128),
                             osb[q_.s][:, 0:TT - 1, :]).then_inc(out_stored[q_.s], 16)
                sp.dma_start(out[q_.b, full:N, :], osb[q_.s][0:N - full, TT - 1, :]).then_inc(out_stored[q_.s], 16)

            def skew(q_):
                sp.wait_ge(attn_ready, q_.b + 1)
                n = 0
                for half in range(2):
                    while n < (half + 1) * NP // 2:
                        m = min(n // 128 * 128 + 128, n // BT * BT + BT)
                        t, p = n // 128, n % 128
                        dst = bass.AP(band_dram.tensor, q_.s * NP * HEADS * 128 + n * HEADS * 128 + n % BT,
                                      [[HEADS * 128 + 1, m - n], [128, HEADS], [1, DENSE]])
                        sp.dma_start(dst, attn[q_.s][p:p + m - n, t, :, 0:DENSE])\
                            .then_inc(band_out[half][q_.s], 16)
                        n = m
                after(sp, bandT_mm, 2 * NB * q_.b)
                for half in range(2):
                    sp.wait_ge(band_out[half][q_.s], 48 * (q_.g + 1))
                    sp.dma_start(band[:, half * NB // 2:(half + 1) * NB // 2, :],
                                 band_dram[q_.s, half * NP // 2:(half + 1) * NP // 2, :]
                                 .rearrange("(t p) w -> p t w", p=BT)).then_inc(band_in[half], 16)

            load_x(Seq(0, 0, 0))
            sp.dma_start(par[:, cut:PCOLS], params[:, cut:PCOLS]).then_inc(par_in, 16)
            sp.dma_start(attn[0][:, :, :, :].rearrange("p t h o -> p (t h o)")[:, 0:ALLCOLS - PCOLS],
                         params[:, PCOLS:ALLCOLS]).then_inc(par_in, 16)
            load_x(Seq(1, 1, 0))
            sp.wait_ge(pads_zero, 1)
            for s in range(2):
                for t in range(TT):
                    sp.dma_start(band_dram[s, 128 * t:128 * t + 128, :], v2[:, :, :, :].rearrange("p t h c -> p (t h c)")).then_inc(scratch_zero, 16)
            sp.wait_ge(scratch_zero, 16 * 2 * TT)

            def turn(T, S_, W):
                if T is not None and not (isinstance(T.b, int) and T.b < 2):
                    load_x(T)
                if S_ is not None:
                    skew(S_)
                if W is not None:
                    store_out(W)
            pipeline(sp, turn, lags=(0, 2, 4))
            sp.wait_ge(out_stored[0], 32 * BATCH // 2)
            sp.wait_ge(out_stored[1], 32 * BATCH // 2)

        @block.tensor
        def _(pe):
            mm, tr = nc.tensor.matmul, nc.tensor.transpose
            ident = P("ident")
            pe.wait_ge(zeros_ready, 1)
            for _ in range(5):
                mm(T1[:, 0:KPAD], k[0][:, 0:128], k[0][:, 0:KPAD], start=True, stop=True)
            pe.wait_ge(conv_in, 16)

            def project_qk(q_):
                if is_first(q_):
                    pe.wait_ge(setup_dve, 1)
                    pe.wait_ge(pads_zero, 1)
                pe.wait_ge(xn_ready, q_.b + 1)
                mm(T1[:, 0:N], P("qkv", 0, D), xn[q_.s][:, :], start=True, stop=True).then_inc(q_mm, 1)
                mm(T0[:, 0:N], P("qkv", D, 2 * D), xn[q_.s][:, :], start=True, stop=True).then_inc(k_mm, 1)

            def project_v(q_):
                pe.wait_ge(q_ready, q_.b + 1)
                mm(T1[:, 0:N], P("qkv", 2 * D, 3 * D), xn[q_.s][:, :], start=True, stop=True).then_inc(v_mm, 1)

            def project_gate(q_):
                pe.wait_ge(v_ready, q_.b + 1)
                mm(T1[:, 0:N], P("gatew"), xn[q_.s][:, :], start=True, stop=True).then_inc(gate_mm, 1)

            def turn_x(q_):
                pe.wait_ge(x_in[q_.s], 16 * (q_.g + 1))
                after(pe, k_ready, q_.b)
                for t in range(3):
                    last = tr(T0[:, t * XT:(t + 1) * XT], xin[q_.s][:, t, :], ident[0:XT, 0:XT])
                last.then_inc(x_turned, 1)

            def convolve(q_, g):
                pe.wait_ge((xT_ready, z_ready, f_ready)[g], q_.b + 1)
                mm(T0[:, 0:N], P("conv", 2 * g * D, (2 * g + 1) * D), xT[:, 0:N], start=True, stop=False)
                mm(T0[:, 0:N], P("conv", (2 * g + 1) * D, (2 * g + 2) * D), xT[:, 1:N + 1],
                   start=False, stop=True).then_inc((z_mm, f_mm, o_mm)[g], 1)

            def center(q_, F):
                if is_first(q_):
                    pe.wait_ge(par_in, 32)
                if F:
                    pe.wait_ge(gelu_ready, FC * (F.b + 1))
                pe.wait_ge(h_ready, q_.b + 1)
                mm(T0[:, 0:N], P("cen4"), h[q_.s][:, :], start=True, stop=True).then_inc(hc_mm, 1)

            def variance(q_, S_):
                if S_:
                    pe.wait_ge(gate_ready, S_.b + 1)
                pe.wait_ge(sq_ready, q_.b + 1)
                mm(T1[:, 0:N], P("avg"), stat[:, :], start=True, stop=True).then_inc(var_mm, 1)

            def score(q_, c, steps):
                if c < CH:
                    src, ready, used, n, end = prod[c], prod_ready[c], prod_used[c], CW // CG, CW
                else:
                    src, ready, used, n, end = fprod, fprod_ready, fprod_used, LSTEPS, LAST
                if c == 0:
                    after(pe, sc_ready, TT * q_.b)
                for r in steps:
                    if c == CH:
                        if r == 0:
                            pe.wait_ge(ready, q_.b + 1)
                    elif c == CH - 1 and r in POOL_PARTS:
                        pe.wait_ge(pool_prod_ready, len(POOL_PARTS) * q_.b + POOL_PARTS.index(r) + 1)
                    elif c == CH - 1:
                        pe.wait_ge(ready, (PARTS - len(POOL_PARTS)) * q_.b + r + 1)
                    else:
                        pe.wait_ge(ready, PARTS * q_.b + r + 1)
                    for g in range(CG):
                        j = n * g + r
                        if j < end:
                            last = mm(S[c][32 * g:32 * g + 32, 0:N], ew[:, c * CW + j, :], src[:, j, :],
                                      start=(r == 0), stop=(r == min(n, end - n * g) - 1))
                if n - 1 in steps:
                    last.then_inc(used, 1)

            def turn_scores(q_):
                pe.wait_ge(scT_ready, (CH + 1) * (q_.b + 1))
                pick_rows = bass.AP(par[:, :].tensor, COL["ident"][0], [[PCOLS, 128], [32, CG], [8, LSTEPS], [1, 8]])
                width = CG * LSTEPS * 8
                for t in range(TT):
                    tok = slice(t * 128, (t + 1) * 128)
                    for c in range(CH):
                        tr(S[t][:, c * 128:(c + 1) * 128], scT[:, c, tok], ident)
                    mm(S[t][:, CH * 128:CH * 128 + width], scT[:, CH, tok], pick_rows, start=True, stop=True)\
                        .then_inc(scores_mm, 1)

            def turn_values(q_):
                after(pe, out_ready, TT * (q_.b - 1))
                for t in range(NB):
                    last = tr(V0[:, t * 128:(t + 1) * 128], vT[q_.s][:, t * BT:t * BT + 128], ident)
                last.then_inc(vwin_mm, 1)

            def far_weights(q_):
                after(pe, x2_ready, q_.b)
                pe.wait_ge(far3_ready, q_.b + 1)
                for t in range(TT):
                    for e in range(2):
                        last = tr(V1b[0:3 * FH, e * 512 + t * 128:e * 512 + (t + 1) * 128],
                                  far3[:, 2 * t + e, :, :].rearrange("p a f -> p (a f)"), identb[:, :])
                last.then_inc(far_mm, 1)

            def spread_far(q_, pair):
                if pair == 0:
                    pe.wait_ge(v2_ready, q_.b + 1)
                    pe.wait_ge(farT_ready, q_.b + 1)
                for e in range(2):
                    i = 2 * pair + e
                    o = FAR[i]
                    if pair > 0:
                        pe.wait_ge(bc_used, NFAR * q_.b + i - 1)
                    mm((V0, V1)[e][:, o:N], pickb[0:3 * FH, i * 128:(i + 1) * 128],
                       farT[:, e, o:N], start=True, stop=True).then_inc(bc_mm, 1)

            def attend(q_, between):
                def turn_band(t):
                    if t % (NB // 2) == 0:
                        pe.wait_ge(band_in[t // (NB // 2)], 16 * (q_.b + 1))
                    for half in range(2):
                        if t == 0:
                            pe.wait_ge(bc_used, NFAR * q_.b + NFAR - 1 + half)
                        else:
                            pe.wait_ge(bandT_ready, 2 * NB * q_.b + 2 * t - 1 + half)
                        for i in range(4):
                            col = (4 * half + i) * 128
                            last = tr((V0, V1)[half][:, i * BT:(i + 1) * BT], band[:, t, col:col + 128],
                                      ident[0:BT, 0:BT])
                        last.then_inc(bandT_mm, 1)

                turn_band(0)
                after(pe, room_ready, q_.b)
                for t in range(NB):
                    between(t)
                    if t + 1 < NB:
                        turn_band(t + 1)
                    pe.wait_ge(bandT_ready, 2 * NB * q_.b + 2 * t + 2)
                    for hh in (0, 2, 4, 6, 1, 3, 5, 7):
                        rows = 32 * (hh // 2)
                        last = mm(V2[rows:rows + 32, t * BT:(t + 1) * BT], v2[:, t, hh, :],
                                  bandT[2 * (t % 2) + hh // 4][:, hh % 4 * BT:(hh % 4 + 1) * BT],
                                  start=(hh % 2 == 0), stop=(hh % 2 == 1))
                    last.then_inc(pv_mm, 1)

            def out_project(q_):
                pe.wait_ge(ao_ready, q_.b + 1)
                mm(V0[:, 0:N], P("outw"), ao[:, :], start=True, stop=True).then_inc(out_mm, 1)

            def center2(q_):
                pe.wait_ge(h2_ready, q_.b + 1)
                mm(V1[:, 0:N], P("cen"), h2[q_.s][:, 0:N], start=True, stop=True).then_inc(hc2_mm, 1)

            def variance2(q_):
                pe.wait_ge(sq2_ready, q_.b + 1)
                mm(V0[:, 0:N], P("avg"), stat2[:, :], start=True, stop=True).then_inc(var2_mm, 1)

            def logits(q_):
                pe.wait_ge(x2_ready, q_.b + 1)
                after(pe, y1_ready, q_.b)
                for t in range(TT):
                    last = mm(V2[:, t * EXPERTS:(t + 1) * EXPERTS], x2[:, t * 128:(t + 1) * 128], P("router"),
                              start=True, stop=True)
                last.then_inc(logit_mm, 1)

            def up(q_, f, T, S_):
                if f == 0:
                    after(pe, gelu_ready, FC * q_.b)
                    if S_:
                        pe.wait_ge(gate_ready, S_.b + 1)
                elif up_bank(f, T) is T1:
                    pe.wait_ge(gelu_ready, FC * q_.b + f - (0 if T else 1))
                elif T:
                    pe.wait_ge(o_ready, T.b + 1)
                elif f == 1:
                    if S_:
                        pe.wait_ge(k_ready, S_.b + 1)
                else:
                    pe.wait_ge(gelu_ready, FC * q_.b + f - 1)
                mm(up_bank(f, T)[:, 0:N], P("up", f * 128, (f + 1) * 128), x2[:, 0:N],
                   start=True, stop=True).then_inc(up_mm, 1)

            def positions(q_):
                pe.wait_ge(msk_ready, q_.b + 1)
                pos = TT * EXPERTS
                for t in range(TT):
                    dst = V2[:, pos + t * EXPERTS:pos + (t + 1) * EXPERTS]
                    for u in range(t):
                        mm(dst, onesb[:, :], msk[:, u, :], start=(u == 0), stop=False)
                    mm(dst, beforeb[:, :], msk[:, t, :], start=(t == 0), stop=True)
                for t in range(TT):
                    rows = min(128, N - t * 128)
                    last = mm(V2[:, 2 * pos:2 * pos + EXPERTS], onesb[0:rows, :], msk[0:rows, t, :],
                              start=(t == 0), stop=(t == TT - 1))
                last.then_inc(pos_mm, 1)

            def down(q_, V, tiles):
                if 0 in tiles:
                    if V:
                        pe.wait_ge(o1_ready, V.b + 1)
                    else:
                        pe.wait_ge(room_ready, q_.b + 1)
                    pe.wait_ge(gelu_ready, FC * (q_.b + 1))
                for t in tiles:
                    for f in range(FC):
                        last = mm(V2[:, t * D:(t + 1) * D], hid[:, f, t * 128:(t + 1) * 128],
                                  P("down", f * D, (f + 1) * D), start=(f == 0), stop=(f == FC - 1))
                if TT - 1 in tiles:
                    last.then_inc(down_mm, 1)

            def turn_h2(q_, F):
                if F:
                    pe.wait_ge(lnv2_ready, F.b + 1)
                else:
                    pe.wait_ge(out_ready, TT * q_.b)
                for t in range(TT):
                    last = tr(V0[:, t * 128:(t + 1) * 128], h2[q_.s][:, t * 128:(t + 1) * 128], ident)
                last.then_inc(h2_turned, 1)

            def turn(T, S_, V, F, W):
                if T:
                    turn_x(T)
                if W:
                    down(W, None, range(2, TT))
                    turn_h2(W, F)
                if S_:
                    project_v(S_)
                if T:
                    convolve(T, 0)
                if S_:
                    project_gate(S_)
                if F:
                    logits(F)
                if S_:
                    score(S_, 0, range(1))
                if F:
                    up(F, 0, T, S_)
                if T:
                    convolve(T, 1)
                if F:
                    up(F, 1, T, S_)
                if V:
                    turn_values(V)
                if T:
                    convolve(T, 2)
                if F:
                    up(F, 2, T, S_)
                if F and not T:
                    up(F, 3, T, S_)
                if V:
                    far_weights(V)
                if S_:
                    score(S_, 0, range(1, 2))
                if F and T:
                    up(F, 3, T, S_)
                if V:
                    spread_far(V, 0)
                if F:
                    positions(F)
                if S_:
                    score(S_, 0, range(2, 3))
                    score(S_, 2, range(1))
                if V:
                    spread_far(V, 1)
                if T:
                    center(T, F)
                if V:
                    spread_far(V, 2)
                if S_:
                    score(S_, 0, range(3, 4))
                if T:
                    variance(T, S_)

                def between(t):
                    if S_ and t == 0:
                        score(S_, 2, range(1, LSTEPS))
                    if T and t == 1:
                        project_qk(T)
                    if S_ and t >= 2:
                        score(S_, 1, range(t - 2, t - 1))
                if V:
                    attend(V, between)
                else:
                    for t in range(NB):
                        between(t)
                if S_:
                    score(S_, 1, range(2, 4))
                if F:
                    down(F, V, range(1))
                if V:
                    out_project(V)
                if S_:
                    turn_scores(S_)
                if V:
                    center2(V)
                if F:
                    down(F, V, range(1, 2))
                if V:
                    variance2(V)
            pipeline(pe, turn, lags=(0, 1, 2, 3, 4))

        @block.scalar
        def _(act):
            A = nc.scalar.activation

            def bias(c):
                return P("bias", c, c + 1)
            act.preload_act_table_set("gelu_and_others")
            act.wait_ge(hbias_ready, 1)

            def copy_qk(q_):
                act.wait_ge(q_mm, q_.b + 1)
                after(act, fprod_used, q_.b - 1)
                A(q[q_.s][:, :], T1[:, 0:N], ACT.Identity, bias=bias(BQ)).then_inc(q_ready, 1)
                act.wait_ge(k_mm, q_.b + 1)
                A(k[q_.s][:, KPAD:KPAD + N], T0[:, 0:N], ACT.Identity, bias=bias(BK)).then_inc(k_ready, 1)

            def copy_v(q_):
                act.wait_ge(v_mm, q_.b + 1)
                after(act, ao_ready, q_.b - 1)
                A(vT[q_.s][:, LOCAL:LOCAL + N], T1[:, 0:N], ACT.Identity, bias=bias(BV)).then_inc(v_ready, 1)

            def tanh_gate(q_):
                act.wait_ge(gate_mm, q_.b + 1)
                A(gate[q_.s][:, :], T1[:, 0:N], ACT.Tanh, bias=hbias[:, BG:BG + 1], scale=0.5)\
                    .then_inc(gate_ready, 1)

            def copy_x(q_):
                act.wait_ge(x_turned, q_.b + 1)
                after(act, o_mm, q_.b)
                A(xT[:, 0:ROWS], T0[:, 0:ROWS], ACT.Copy).then_inc(xT_ready, 1)

            def tanh_z(q_):
                act.wait_ge(z_mm, q_.b + 1)
                after(act, h_ready, q_.b)
                A(zt[:, :], T0[:, 0:N], ACT.Tanh, bias=bias(BZ)).then_inc(z_ready, 1)

            def tanh_f(q_):
                act.wait_ge(f_mm, q_.b + 1)
                A(ft[:, :], T0[:, 0:N], ACT.Tanh, bias=hbias[:, BF:BF + 1], scale=0.5).then_inc(f_ready, 1)

            def tanh_o(q_):
                act.wait_ge(o_mm, q_.b + 1)
                A(ot[:, :], T0[:, 0:N], ACT.Tanh, bias=hbias[:, BO:BO + 1], scale=0.5).then_inc(o_ready, 1)

            def norm_square(q_):
                if is_first(q_):
                    act.wait_ge(pads_zero, 1)
                act.wait_ge(hc_mm, q_.b + 1)
                after(act, xn_ready, q_.b)
                A(stat[:, :], T0[:, 0:N], ACT.Square).then_inc(sq_ready, 1)

            def norm1_ln(q_):
                act.wait_ge(var_mm, q_.b + 1)
                A(stat[:, :], T1[:, 0:N], ACT.Ln, bias=epsc[:, 0:1]).then_inc(lnv_ready, 1)

            def norm1_exp(q_):
                act.wait_ge(lnv_ready, q_.b + 1)
                A(stat[:, :], stat[:, :], ACT.Exp, scale=-0.5).then_inc(rstd_ready, 1)

            def norm2_square(q_):
                act.wait_ge(hc2_mm, q_.b + 1)
                after(act, x2_ready, q_.b)
                A(stat2[:, :], V1[:, 0:N], ACT.Square).then_inc(sq2_ready, 1)

            def norm2(q_):
                act.wait_ge(var2_mm, q_.b + 1)
                A(stat2[:, :], V0[:, 0:N], ACT.Ln, bias=epsc[:, 0:1]).then_inc(lnv2_ready, 1)
                act.wait_ge(lnv2_ready, q_.b + 1)
                A(stat2[:, :], stat2[:, :], ACT.Exp, scale=-0.5).then_inc(rstd2_ready, 1)

            def softmax_exp(q_):
                act.wait_ge(sub_ready, q_.b + 1)
                after(act, attn_ready, q_.b)
                A(ex[:, :, :], sc[:, :, :], ACT.Exp).then_inc(ex_ready, 1)

            def score_copy(q_, c):
                act.wait_ge(prod_used[c] if c < CH else fprod_used, q_.b + 1)
                after(act, scores_mm, TT * q_.b)
                A(scT[:, c, 0:N], S[c][:, 0:N], ACT.Copy).then_inc(scT_ready, 1)

            def value_blocks(q_):
                act.wait_ge(vwin_mm, q_.b + 1)
                after(act, pv_mm, NB * q_.b)
                for t in range(NB):
                    dst = bass.AP(v2[:, :, :, :].tensor, t * HEADS * 32,
                                  [[NB * HEADS * 32, 128], [64, HEADS // 2], [32 + HD, 2], [1, HD]])
                    last = A(dst, V0[:, t * 128:(t + 1) * 128].rearrange("p (i e d) -> p i e d", e=2, d=HD), ACT.Copy)
                last.then_inc(v2_ready, 1)

            def far_copy(q_):
                act.wait_ge(far_mm, q_.b + 1)
                after(act, bc_mm, NFAR * q_.b)
                A(farT[:, :, :], V1b[0:3 * FH, :].rearrange("p (e n) -> p e n", e=2)[:, :, 0:NP], ACT.Copy)\
                    .then_inc(farT_ready, 1)

            def band_copies(q_, groups):
                for g in groups:
                    act.wait_ge(bandT_mm, 2 * NB * q_.b + g + 1)
                    after(act, pv_mm, NB * q_.b + g // 2 - 1)
                    A(bandT[g % 4][:, :], (V0, V1)[g % 2][:, 0:4 * BT], ACT.Copy).then_inc(bandT_ready, 1)

            def router_exp(q_):
                act.wait_ge(lsub_ready, q_.b + 1)
                after(act, gs_ready, q_.b)
                A(exr[:, :, :], lsub[:, :, :], ACT.Exp).then_inc(exr_ready, 1)

            def gelu(q_, f, T):
                if f == 0:
                    after(act, down_mm, q_.b)
                act.wait_ge(up_mm, FC * q_.b + f + 1)
                A(hid[:, f, 0:N], up_bank(f, T)[:, 0:N], ACT.Gelu, bias=bias(B1 + f))\
                    .then_inc(gelu_ready, 1)

            def turn(T, S_, V, F):
                if T:
                    copy_x(T)
                if V:
                    softmax_exp(V)
                if S_:
                    copy_v(S_)
                act.preload_act_table_set("gelu_and_others")
                if T:
                    tanh_z(T)
                if S_:
                    tanh_gate(S_)
                if F:
                    gelu(F, 0, T)
                if T:
                    tanh_f(T)
                if F:
                    gelu(F, 1, T)
                if V:
                    value_blocks(V)
                if T:
                    tanh_o(T)
                if F:
                    gelu(F, 2, T)
                if F and not T:
                    gelu(F, 3, T)
                if V:
                    far_copy(V)
                if F and T:
                    gelu(F, 3, T)
                act.preload_act_table_set("natural_log_exp_and_others")
                if F:
                    router_exp(F)
                if T:
                    norm_square(T)
                if S_:
                    score_copy(S_, 0)
                if T:
                    norm1_ln(T)
                if V:
                    band_copies(V, range(2))
                if T:
                    norm1_exp(T)
                if S_:
                    score_copy(S_, 2)
                if V:
                    band_copies(V, range(2, 4))
                if T:
                    copy_qk(T)
                if V:
                    band_copies(V, range(4, 2 * NB))
                if S_:
                    score_copy(S_, 1)
                if V:
                    norm2_square(V)
                    norm2(V)
            pipeline(act, turn)

        @block.vector
        def _(dve):
            v = nc.vector
            v.memset(epsc[:, :], EPS)
            dve.wait_ge(conv_in, 16)
            v.tensor_scalar(hbias[:, :], P("bias"), 0.5, None, ALU.mult).then_inc(hbias_ready, 1)
            def setup():
                dve.wait_ge(par_in, 32)
                v.memset(room[:, :], float(CAP))
                v.tensor_copy(beforeb[:, :], P("before"))
                v.tensor_copy(onesb[:, :], P("ones"))
                v.tensor_copy(identb[:, :], P("ident"))
                v.tensor_copy(pickb[:, :], P("pick"))
                v.tensor_scalar(gain2[:, :], P("gain"), 0.5, None, ALU.mult)
                v.tensor_scalar(se1[:, :], P("se"), 1.0, HD ** -0.5, ALU.add, ALU.mult).then_inc(setup_lin, 1)
                dve.wait_ge(setup_lin, 1)
                for first, end, steps in ((0, CH * CW, CW // CG), (CH * CW, NO, LSTEPS)):
                    for r in range(steps):
                        n = (end - first - r + steps - 1) // steps
                        o = first + r
                        v.tensor_tensor(bass.AP(ew[:, :, :].tensor, o * 32, [[NO * 32, 128], [steps * 32, n], [1, 32]]),
                                        bass.AP(se1[:, :].tensor, o, [[NO, 128], [steps, n], [0, 32]]),
                                        P("ind", r * 32, (r + 1) * 32).unsqueeze(1).broadcast_to([128, n, 32]), ALU.mult)
                oh = P("cosk").rearrange("p (h o) -> p h o", o=NO)
                v.tensor_tensor(bias_oh, oh, P("amp").unsqueeze(2).broadcast_to([128, HEADS, NO]), ALU.mult)\
                    .then_inc(setup_lin, 1)
                dve.wait_ge(setup_lin, 2)
                v.tensor_tensor(bias_oh, bias_oh, P("pos").rearrange("p (h o) -> p h o", o=NO), ALU.add)\
                    .then_inc(setup_lin, 1)
                dve.wait_ge(setup_lin, 3)
                for t in range(TT):
                    last = v.tensor_tensor(bm[:, t, :, :], bias_oh,
                                           P("mask", t * NO, (t + 1) * NO).unsqueeze(1).broadcast_to([128, HEADS, NO]),
                                           ALU.add)
                last.then_inc(setup_dve, 1)
                dve.wait_ge(setup_dve, 1)
                dve.wait_ge(pads_zero, 1)

            def recur(q_):
                dve.wait_ge(z_ready, q_.b + 1)
                dve.wait_ge(f_ready, q_.b + 1)
                v.tensor_scalar(forget[:, :], ft[:, :], 0.5, 0.5, ALU.mult, ALU.add)
                v.scalar_tensor_tensor(mixin[:, :], ft[:, :], 1.0, zt[:, :], ALU.subtract, ALU.mult)\
                    .then_inc(mixin_ready, 1)
                dve.wait_ge(mixin_ready, q_.b + 1)
                v.tensor_tensor_scan(cell[:, :], forget[:, :], mixin[:, :], 0.0, ALU.mult, ALU.add)\
                    .then_inc(c_ready, 1)
                dve.wait_ge(c_ready, q_.b + 1)
                dve.wait_ge(o_ready, q_.b + 1)
                after(dve, hkeep_ready, q_.b - 1)
                v.scalar_tensor_tensor(h[q_.s][:, :], ot[:, :], 1.0, cell[:, :], ALU.add, ALU.mult)\
                    .then_inc(h_ready, 1)

            def norm1(q_):
                dve.wait_ge(rstd_ready, q_.b + 1)
                after(dve, gate_ready, q_.b - 1)
                v.tensor_tensor(xn[q_.s][:, :], T0[:, 0:N], stat[:, :], ALU.mult).then_inc(xn_ready, 1)

            def products(q_, c, part):
                if part == 0:
                    dve.wait_ge(k_ready, q_.b + 1)
                    after(dve, prod_used[c], q_.b)
                w = CW // PARTS
                back = bass.AP(k[q_.s][:, :].tensor, KPAD - LOCAL + c * CW + part,
                               [[KPAD + NP, 128], [PARTS, w], [1, N]])
                v.tensor_tensor(bass.AP(prod[c][:, :, :].tensor, part * N, [[CW * N, 128], [PARTS * N, w], [1, N]]),
                                q[q_.s][:, :].unsqueeze(1).broadcast_to([128, w, N]), back,
                                ALU.mult).then_inc(prod_ready[c], 1)

            def softmax_in(q_):
                for t in range(TT):
                    dve.wait_ge(scores_mm, TT * q_.b + t + 1)
                    v.tensor_tensor(sc[:, t * HEADS:(t + 1) * HEADS, :],
                                    S[t][:, 0:SC].rearrange("p (o h) -> p h o", h=HEADS), bm[:, t, :, :],
                                    ALU.add).then_inc(sc_ready, 1)
                dve.wait_ge(sc_ready, TT * (q_.b + 1))
                v.tensor_reduce(mx[:, :], sc[:, :, :], AX.X, ALU.max).then_inc(mx_ready, 1)
                dve.wait_ge(mx_ready, q_.b + 1)
                v.tensor_tensor(sc[:, :, :], sc[:, :, :], mx[:, :].unsqueeze(2).broadcast_to([128, TT * HEADS, NO]),
                                ALU.subtract).then_inc(sub_ready, 1)

            def softmax_out(q_):
                dve.wait_ge(ex_ready, q_.b + 1)
                v.tensor_reduce(sm[:, :], ex[:, :, :], AX.X, ALU.add).then_inc(sm_ready, 1)
                dve.wait_ge(sm_ready, q_.b + 1)
                v.reciprocal(rs[:, :], sm[:, :]).then_inc(rc_ready, 1)
                dve.wait_ge(rc_ready, q_.b + 1)
                rs3 = rs[:, :].rearrange("p (t h) -> p t h", h=HEADS)
                v.tensor_tensor(rs3, rs3, gain2[:, :].unsqueeze(1).broadcast_to([128, TT, HEADS]), ALU.mult)\
                    .then_inc(rs_ready, 1)
                dve.wait_ge(rs_ready, q_.b + 1)
                after(dve, band_out[0][q_.s], 48 * q_.g)
                after(dve, band_out[1][q_.s], 48 * q_.g)
                after(dve, far3_ready, q_.b)
                v.tensor_tensor(attn[q_.s][:, :, :, :].rearrange("p t h o -> p (t h) o"), ex[:, :, 0:DENSE],
                                rs[:, :].unsqueeze(2).broadcast_to([128, TT * HEADS, DENSE]), ALU.mult)\
                    .then_inc(attn_ready, 1)
                half = NFAR // 2
                for e in range(2):
                    last = v.tensor_tensor(
                        bass.AP(attnf[:, :, :].tensor, FH * e, [[TT * 2 * FH, 128], [2 * FH, TT], [half, HEADS], [1, half]]),
                        bass.AP(ex[:, :, :].tensor, DENSE + e,
                                [[TT * HEADS * NO, 128], [HEADS * NO, TT], [NO, HEADS], [2, half]]),
                        rs3.unsqueeze(3).broadcast_to([128, TT, HEADS, half]), ALU.mult)
                last.then_inc(attnf_ready, 1)

            def far_values(q_, pair):
                for i in (2 * pair, 2 * pair + 1):
                    o = FAR[i]
                    dve.wait_ge(bc_mm, NFAR * q_.b + i + 1)
                    if 1 <= i:
                        after(dve, acc_added, (NFAR - 1) * q_.b + (i - 2 if i > 2 else 0))
                    dst = acc if i == 0 else tmp[i % 2]
                    v.tensor_tensor(dst[:, o:N], (V0, V1)[i % 2][:, o:N], vT[q_.s][:, LOCAL:LOCAL + N - o],
                                    ALU.mult).then_inc(bc_used, 1)

            def attention_out(q_):
                dve.wait_ge(pv_mm, NB * (q_.b + 1))
                dve.wait_ge(acc_added, (NFAR - 1) * (q_.b + 1))
                v.tensor_tensor(o1[:, :], V2[:, 0:N], acc[:, :], ALU.add).then_inc(o1_ready, 1)
                dve.wait_ge(o1_ready, q_.b + 1)
                v.scalar_tensor_tensor(ao[:, :], gate[q_.s][:, :], 1.0, o1[:, :], ALU.add, ALU.mult)\
                    .then_inc(ao_ready, 1)

            def residual(q_):
                dve.wait_ge(out_mm, q_.b + 1)
                dve.wait_ge(hkeep_ready, q_.b + 1)
                after(dve, h2_turned, q_.b - 1)
                v.scalar_tensor_tensor(h2[q_.s][:, 0:N], V0[:, 0:N], P("bias", BOUT, BOUT + 1), hkeep[q_.s][:, :],
                                       ALU.add, ALU.add).then_inc(h2_ready, 1)

            def norm2(q_):
                dve.wait_ge(rstd2_ready, q_.b + 1)
                after(dve, up_mm, FC * q_.b)
                v.tensor_tensor(x2[:, 0:N], V1[:, 0:N], stat2[:, :], ALU.mult).then_inc(x2_ready, 1)

            def route(q_):
                dve.wait_ge(logit_mm, q_.b + 1)
                v.tensor_copy(lg[:, :, :], V2[:, 0:TT * EXPERTS].rearrange("p (t e) -> p t e", e=EXPERTS))\
                    .then_inc(lg_ready, 1)
                dve.wait_ge(lg_ready, q_.b + 1)
                v.tensor_reduce(lmax[:, :], lg[:, :, :], AX.X, ALU.max).then_inc(lmax_ready, 1)
                for t in range(TT):
                    last = v.max(m8[:, t, :], lg[:, t, :])
                last.then_inc(m8_ready, 1)
                dve.wait_ge(lmax_ready, q_.b + 1)
                dve.wait_ge(m8_ready, q_.b + 1)
                v.tensor_tensor(lsub[:, :, :], lg[:, :, :], lmax[:, :].unsqueeze(2).broadcast_to([128, TT, EXPERTS]),
                                ALU.subtract).then_inc(lsub_ready, 1)

            def route_picks(q_):
                for t in range(TT):
                    last = v.max_index(i8[:, t, :], m8[:, t, :], lg[:, t, :])
                last.then_inc(i8_ready, 1)
                dve.wait_ge(i8_ready, q_.b + 1)
                v.tensor_copy(idf[:, :, :], i8[:, :, 0:TOPK]).then_inc(idf_ready, 1)
                dve.wait_ge(idf_ready, q_.b + 1)
                iota = P("iota").unsqueeze(1).broadcast_to([128, TT, EXPERTS])
                v.tensor_tensor(eq0[:, :, :], iota, idf[:, :, 0:1].broadcast_to([128, TT, EXPERTS]), ALU.is_equal)
                v.tensor_tensor(eq1[:, :, :], iota, idf[:, :, 1:2].broadcast_to([128, TT, EXPERTS]), ALU.is_equal)\
                    .then_inc(eq_ready, 1)
                dve.wait_ge(eq_ready, q_.b + 1)
                v.tensor_tensor(msk[:, :, :], eq0[:, :, :], eq1[:, :, :], ALU.add).then_inc(msk_ready, 1)

            def keep(q_):
                dve.wait_ge(pos_mm, q_.b + 1)
                v.tensor_tensor(kept[:, :, :], V2[:, TT * EXPERTS:2 * TT * EXPERTS].rearrange("p (t e) -> p t e", e=EXPERTS),
                                room[:, :].unsqueeze(1).broadcast_to([128, TT, EXPERTS]), ALU.is_lt)\
                    .then_inc(kept_ready, 1)
                dve.wait_ge(kept_ready, q_.b + 1)
                v.tensor_tensor(room[:, :], room[:, :], V2[:, 2 * TT * EXPERTS:(2 * TT + 1) * EXPERTS], ALU.subtract)\
                    .then_inc(room_ready, 1)

            def weigh(q_):
                dve.wait_ge(exr_ready, q_.b + 1)
                v.tensor_reduce(smr[:, :], exr[:, :, :], AX.X, ALU.add).then_inc(smr_ready, 1)
                dve.wait_ge(kw_ready, q_.b + 1)
                v.tensor_reduce(gs[:, :], kw[:, :, :], AX.X, ALU.add)
                dve.wait_ge(smr_ready, q_.b + 1)
                v.reciprocal(rcr[:, :], smr[:, :]).then_inc(gs_ready, 1)
                dve.wait_ge(gs_ready, q_.b + 1)
                v.tensor_tensor(gt[:, :], gs[:, :], rcr[:, :], ALU.mult).then_inc(gt_ready, 1)

            def finish(q_):
                dve.wait_ge(down_mm, q_.b + 1)
                v.tensor_tensor(y1[:, :, :], V2[:, 0:TT * D].rearrange("p (t d) -> p t d", d=D),
                                P("b2").unsqueeze(1).broadcast_to([128, TT, D]), ALU.add).then_inc(y1_ready, 1)
                dve.wait_ge(y1_ready, q_.b + 1)
                dve.wait_ge(gt_ready, q_.b + 1)
                dve.wait_ge(h2_turned, q_.b + 1)
                after(dve, out_stored[q_.s], 32 * q_.g)
                for t in range(TT):
                    v.scalar_tensor_tensor(osb[q_.s][:, t, :], y1[:, t, :], gt[:, t:t + 1],
                                           V0[:, t * D:(t + 1) * D], ALU.mult, ALU.add).then_inc(out_ready, 1)

            def turn(T, S_, V, F):
                if V:
                    softmax_out(V)
                if F:
                    route(F)
                    route_picks(F)
                if T:
                    recur(T)
                if T and is_first(T):
                    setup()
                if V:
                    far_values(V, 0)
                if F:
                    keep(F)
                if V:
                    far_values(V, 1)
                    far_values(V, 2)
                if S_:
                    products(S_, 1, 0)
                if T:
                    norm1(T)
                if S_:
                    products(S_, 1, 1)
                if F:
                    weigh(F)
                if T:
                    products(T, 0, 0)
                    products(T, 0, 1)
                if V:
                    attention_out(V)
                if T:
                    products(T, 0, 2)
                if V:
                    residual(V)
                if S_:
                    softmax_in(S_)
                if T:
                    products(T, 0, 3)
                if V:
                    norm2(V)
                if F:
                    finish(F)
            pipeline(dve, turn)

        @block.gpsimd
        def _(pool):
            g = nc.gpsimd
            for s in range(2):
                last = g.memset(k[s][:, 0:KPAD], 0.0)
                if s == 0:
                    last.then_inc(zeros_ready, 1)
                g.memset(vT[s][:, 0:LOCAL], 0.0)
                g.memset(vT[s][:, LOCAL + N:LOCAL + NP], 0.0)
                g.memset(h2[s][:, N:NP], 0.0)
            g.memset(scT[:, :, N:NP], 0.0)
            for i, o in enumerate(FAR):
                g.memset(fprod[:, i + 1, 0:o], 0.0)
            g.memset(acc[:, 0:FAR[0]], 0.0)
            g.memset(one[:, :], 1.0)
            g.memset(back4[:, :], -0.25)
            g.memset(x2[:, N:NP], 0.0)
            g.memset(hid[:, :, N:NP], 0.0)
            g.memset(v2[:, :, :, :], 0.0).then_inc(pads_zero, 1)
            pool.wait_ge(pads_zero, 1)

            def carry(q_):
                pool.wait_ge(h_ready, q_.b + 1)
                after(pool, h2_ready, q_.b - 1)
                g.tensor_tensor(hkeep[q_.s][:, :], h[q_.s][:, :], back4[:, :].broadcast_to([128, N]), ALU.mult)\
                    .then_inc(hkeep_ready, 1)

            def far_products(q_):
                pool.wait_ge(k_ready, q_.b + 1)
                after(pool, fprod_used, q_.b)
                for i, o in enumerate(OFFS[CH * CW:]):
                    last = g.tensor_tensor(fprod[:, i, o:N], q[q_.s][:, o:N], k[q_.s][:, KPAD:KPAD + N - o], ALU.mult)
                last.then_inc(fprod_ready, 1)

            def local_products(q_):
                c = CH - 1
                pool.wait_ge(k_ready, q_.b + 1)
                after(pool, prod_used[c], q_.b)
                w = CW // PARTS
                for part in POOL_PARTS:
                    back = bass.AP(k[q_.s][:, :].tensor, KPAD - LOCAL + c * CW + part,
                                   [[KPAD + NP, 128], [PARTS, w], [1, N]])
                    g.tensor_tensor(bass.AP(prod[c][:, :, :].tensor, part * N, [[CW * N, 128], [PARTS * N, w], [1, N]]),
                                    q[q_.s][:, :].unsqueeze(1).broadcast_to([128, w, N]), back,
                                    ALU.mult).then_inc(pool_prod_ready, 1)

            def split_far(q_):
                one3 = one[:, :].unsqueeze(2).broadcast_to([128, TT * 2, FH])
                pool.wait_ge(attnf_ready, q_.b + 1)
                after(pool, far_mm, q_.b)
                g.tensor_tensor(far3[:, :, 0, :], attnf[:, :, :], one3, ALU.mult).then_inc(hi_ready, 1)
                pool.wait_ge(hi_ready, q_.b + 1)
                g.tensor_tensor(rest[:, :, :], attnf[:, :, :], far3[:, :, 0, :], ALU.subtract).then_inc(rest_ready, 1)
                pool.wait_ge(rest_ready, q_.b + 1)
                g.tensor_tensor(far3[:, :, 1, :], rest[:, :, :], one3, ALU.mult).then_inc(mid_ready, 1)
                pool.wait_ge(mid_ready, q_.b + 1)
                g.tensor_tensor(far3[:, :, 2, :], rest[:, :, :], far3[:, :, 1, :], ALU.subtract).then_inc(far3_ready, 1)

            def far_sum(q_):
                for i in range(1, NFAR):
                    o = FAR[i]
                    pool.wait_ge(bc_used, NFAR * q_.b + i + 1)
                    after(pool, acc_added, (NFAR - 1) * q_.b + i - 1)
                    g.tensor_tensor(acc[:, o:N], acc[:, o:N], tmp[i % 2][:, o:N], ALU.add).then_inc(acc_added, 1)

            def kept_weights(q_):
                pool.wait_ge(kept_ready, q_.b + 1)
                g.tensor_tensor(kept[:, :, :], kept[:, :, :], msk[:, :, :], ALU.mult).then_inc(kept2_ready, 1)
                pool.wait_ge(kept2_ready, q_.b + 1)
                pool.wait_ge(exr_ready, q_.b + 1)
                g.tensor_tensor(kw[:, :, :], kept[:, :, :], exr[:, :, :], ALU.mult).then_inc(kw_ready, 1)

            def turn(T, S_, V, F):
                if S_:
                    carry(S_)
                    local_products(S_)
                if V:
                    split_far(V)
                    far_sum(V)
                if F:
                    kept_weights(F)
                if T:
                    far_products(T)
            pipeline(pool, turn)


def _params(i):
    f = np.float32
    a = {}
    a["ident"] = np.eye(128, dtype=f)
    a["conv"] = np.concatenate([i["L0_tok_W_" + g][:, :, t].T for g in "zfo" for t in range(2)], axis=1)
    cols = [i["L0_tok_b_" + g][:, None] for g in "zfo"]
    qb = i["L0_attn_b_qkv"]
    cols += [qb[D * t:D * (t + 1), None] for t in range(3)]
    cols += [i["L0_attn_b_gate"][:, None], i["L0_attn_b_out"][:, None], i["L0_ffn_b1"].reshape(FC, 128).T]
    a["bias"] = np.concatenate(cols, axis=1)
    a["cen"] = (np.eye(128) - 1.0 / 128).astype(f)
    a["cen4"] = a["cen"] * f(-0.25)
    a["avg"] = np.full((128, 128), 1.0 / 128, f)
    a["qkv"] = i["L0_attn_W_qkv"]
    a["gatew"] = i["L0_attn_W_gate"]
    order = OFFS_INDEX
    a["se"] = np.tile(i["L0_attn_scale_embed"][order].T, (HEADS, 1))
    ch = np.arange(128)
    col = np.arange(32)[None, None, :]
    a["ind"] = (col == 8 * np.arange(4)[None, :, None] + ch[:, None, None] // HD).astype(f).reshape(128, 128)
    a["pos"] = np.broadcast_to(i["L0_attn_pos_bias"][order].T.reshape(1, SC), (128, SC))
    log_max = np.log(1.0 + 4096.0)
    om = np.array([0.0, 0.0, 1, 1, 4, 4, 6, 6]) * np.pi / log_max
    logd = np.log(1.0 + np.array(OFFS, np.float64))
    cosk = np.where(om[:, None] > 0, np.cos(om[:, None] * logd[None, :]), 0.0).astype(f)
    a["cosk"] = np.broadcast_to(cosk.reshape(1, SC), (128, SC))
    a["amp"] = np.broadcast_to(i["L0_attn_disp_amp"][None, :], (128, HEADS))
    a["gain"] = np.broadcast_to(i["L0_attn_if_gain"][None, :], (128, HEADS))
    tok = ch[:, None, None] + 128 * np.arange(TT)[None, :, None]
    a["mask"] = np.where(tok >= np.array(OFFS)[None, None, :], 0.0, MASKED).astype(f).reshape(128, TT * NO)
    pick = np.zeros((128, NFAR, 128), f)
    for hh in range(HEADS):
        for s in range(NFAR):
            for part in range(3):
                pick[part * FH + hh * (NFAR // 2) + s // 2, s, hh * HD:(hh + 1) * HD] = 1.0
    a["pick"] = pick.reshape(128, NFAR * 128)
    a["outw"] = i["L0_attn_W_out"]
    a["router"] = i["L0_ffn_router_w"].T
    a["up"] = i["L0_ffn_w1"].T
    a["down"] = i["L0_ffn_w2"].T.reshape(FC, 128, D).transpose(1, 0, 2).reshape(128, FC * D)
    a["b2"] = np.broadcast_to(i["L0_ffn_b2"][None, :], (128, D))
    a["iota"] = np.broadcast_to(np.arange(EXPERTS, dtype=f)[None, :], (128, EXPERTS))
    a["before"] = (ch[:, None] < ch[None, :]).astype(f)
    a["ones"] = np.ones((128, 128), f)
    for n, w in FIELDS + SETUP:
        assert a[n].shape == (128, w), (n, a[n].shape)
    return np.ascontiguousarray(np.concatenate([a[n] for n, _ in FIELDS + SETUP], axis=1))


OFFS_INDEX = [LOCAL - j for j in range(DENSE)] + [DENSE + s for s in range(NFAR)]


def kernel(**inputs):
    import concourse.bacc as _bacc
    from concourse.bass_utils import run_bass_kernel_spmd as _run

    i = {n: np.asarray(a) for n, a in inputs.items()}
    arrays = {"x_dram": np.ascontiguousarray(i["x"]), "params_dram": _params(i)}
    nc = _bacc.Bacc("TRN2", target_bir_lowering=False, num_devices=1)
    f32 = mybir.dt.float32
    x = nc.dram_tensor("x_dram", [BATCH, ROWS, D], f32, kind="ExternalInput").ap()
    params = nc.dram_tensor("params_dram", [128, ALLCOLS], f32, kind="ExternalInput").ap()
    out = nc.dram_tensor("out_dram", [BATCH, N, D], f32, kind="ExternalOutput").ap()
    build(nc, x, params, out)
    r = _run(nc, [arrays], core_ids=[0])
    return r.results[0]["out_dram"]
```
